# Optimizing a Trainium2 kernel written in Bass

```python
import numpy as np
import jax
import jax.numpy as jnp

def _softmax(x, axis=-1):
    return jax.nn.softmax(x, axis=axis)

def _gelu(x):
    return jax.nn.gelu(x, approximate=True)

def _silu(x):
    return jax.nn.silu(x)

def _sigmoid(x):
    return jax.nn.sigmoid(x)

def _layernorm(x, axis=-1, eps=1e-05):
    m = jnp.mean(x, axis=axis, keepdims=True)
    v = jnp.var(x, axis=axis, keepdims=True)
    return (x - m) / jnp.sqrt(v + eps)

def _scatter_add(tgt, idx, src, axis=0):
    return tgt.at[idx].add(src)

def _segment_sum(src, seg, n):
    return jax.ops.segment_sum(src, seg, n)
kernel_name = 'mk_sandwich_d1_jaxref_r2_701821'

def setup_inputs(seed: int=0):
    np.random.seed(seed)
    _w = jnp.asarray

    def _L0_attn_setup():
        import jax, jax.numpy as jnp
        import numpy as np
        B, S, H, NH = (8, 2048, 512, 16)
        HD = H // NH
        EPS_ATTN = 1e-06
        EPS_LN = 1e-12
        key = jax.random.key(seed)
        ks = jax.random.split(key, 10)
        s = 1.0 / np.sqrt(H)
        return {'input_tensor': jax.random.normal(ks[0], (B, S, H), dtype=jnp.float32), 'attention_mask': jnp.zeros((B, S), dtype=jnp.int32), 'Wq': jax.random.normal(ks[1], (H, H), dtype=jnp.float32) * s, 'bq': jnp.zeros((H,), dtype=jnp.float32), 'Wk': jax.random.normal(ks[2], (H, H), dtype=jnp.float32) * s, 'bk': jnp.zeros((H,), dtype=jnp.float32), 'Wv': jax.random.normal(ks[3], (H, H), dtype=jnp.float32) * s, 'bv': jnp.zeros((H,), dtype=jnp.float32), 'Wd': jax.random.normal(ks[4], (H, H), dtype=jnp.float32) * s, 'bd': jnp.zeros((H,), dtype=jnp.float32), 'gamma': jnp.ones((H,), dtype=jnp.float32), 'beta': jnp.zeros((H,), dtype=jnp.float32)}
    _L0_attn_in = _L0_attn_setup()

    def _L0_ffn_setup():
        import jax, jax.numpy as jnp
        import numpy as np
        B, N, D = (4, 1024, 512)
        SPARSITY = 0.01
        key = jax.random.key(seed)
        k1, k2, k3 = jax.random.split(key, 3)
        x = jax.random.normal(k1, (B, N, D), dtype=jnp.float32)
        spatial = jax.random.normal(k2, (D, D), dtype=jnp.float32) * 0.02
        freq = jnp.fft.fft(spatial, axis=-1)
        k = int(D * SPARSITY)
        mag = jnp.abs(freq)
        kth = jax.lax.top_k(mag, k)[0][:, -1:]
        w_sparse = jnp.where(mag >= kth, freq, 0.0 + 0j)
        bias = jax.random.normal(k3, (D,), dtype=jnp.float32) * 0.01
        return {'x': x, 'w_freq_real': jnp.real(w_sparse).astype(jnp.float32), 'w_freq_imag': jnp.imag(w_sparse).astype(jnp.float32), 'bias': bias}
    _L0_ffn_in = _L0_ffn_setup()
    _d = {'L0_attn_input_tensor': _L0_attn_in['input_tensor'], 'L0_attn_attention_mask': _L0_attn_in['attention_mask'], 'L0_attn_Wq': _L0_attn_in['Wq'], 'L0_attn_bq': _L0_attn_in['bq'], 'L0_attn_Wk': _L0_attn_in['Wk'], 'L0_attn_bk': _L0_attn_in['bk'], 'L0_attn_Wv': _L0_attn_in['Wv'], 'L0_attn_bv': _L0_attn_in['bv'], 'L0_attn_Wd': _L0_attn_in['Wd'], 'L0_attn_bd': _L0_attn_in['bd'], 'L0_attn_gamma': _L0_attn_in['gamma'], 'L0_attn_beta': _L0_attn_in['beta'], 'L0_ffn_w_freq_real': _L0_ffn_in['w_freq_real'], 'L0_ffn_w_freq_imag': _L0_ffn_in['w_freq_imag'], 'L0_ffn_bias': _L0_ffn_in['bias']}
    _x0 = _d['L0_attn_input_tensor']
    _d['L0_attn_input_tensor'] = jax.random.normal(jax.random.fold_in(jax.random.key(seed), 1), (8, 2048, 512), dtype=_x0.dtype)
    del _x0
    return _d

def reference(L0_attn_input_tensor, L0_attn_attention_mask, L0_attn_Wq, L0_attn_bq, L0_attn_Wk, L0_attn_bk, L0_attn_Wv, L0_attn_bv, L0_attn_Wd, L0_attn_bd, L0_attn_gamma, L0_attn_beta, L0_ffn_w_freq_real, L0_ffn_w_freq_imag, L0_ffn_bias):

    def _L0_attn_ref(input_tensor, attention_mask, Wq, bq, Wk, bk, Wv, bv, Wd, bd, gamma, beta):
        import jax, jax.numpy as jnp
        import numpy as np
        B, S, H, NH = (8, 2048, 512, 16)
        HD = H // NH
        EPS_ATTN = 1e-06
        EPS_LN = 1e-12
        x = input_tensor
        b, s, h = x.shape
        q = (x @ Wq.T + bq).reshape(b, s, NH, HD)
        k = (x @ Wk.T + bk).reshape(b, s, NH, HD)
        v = (x @ Wv.T + bv).reshape(b, s, NH, HD)
        q = jax.nn.elu(q) + 1.0
        k = jax.nn.elu(k) + 1.0
        kv = jnp.einsum('nshd,nshm->nhmd', k, v)
        z = 1.0 / jnp.einsum('nlhd,nhd->nlh', q, k.sum(axis=1) + EPS_ATTN)
        ctx = jnp.einsum('nlhd,nhmd,nlh->nlhm', q, kv, z).reshape(b, s, h)
        hs = ctx @ Wd.T + bd
        hs = hs + x
        mu = hs.mean(axis=-1, keepdims=True)
        var = ((hs - mu) ** 2).mean(axis=-1, keepdims=True)
        out = (hs - mu) / jnp.sqrt(var + EPS_LN) * gamma + beta
        return out

    def _L0_ffn_ref(x, w_freq_real, w_freq_imag, bias):
        import jax, jax.numpy as jnp
        import numpy as np
        B, N, D = (4, 1024, 512)
        SPARSITY = 0.01
        w = jax.lax.complex(w_freq_real, w_freq_imag)
        x_freq = jnp.fft.fft(x, axis=-1)
        y_freq = jnp.einsum('bnd,do->bno', x_freq, w)
        y = jnp.real(jnp.fft.ifft(y_freq, axis=-1))
        return y + bias
    x = L0_attn_input_tensor
    x = x + _layernorm(_L0_attn_ref(_layernorm(x, axis=-1), L0_attn_attention_mask, L0_attn_Wq, L0_attn_bq, L0_attn_Wk, L0_attn_bk, L0_attn_Wv, L0_attn_bv, L0_attn_Wd, L0_attn_bd, L0_attn_gamma, L0_attn_beta), axis=-1)
    x = x + _layernorm(_L0_ffn_ref(_layernorm(x, axis=-1), L0_ffn_w_freq_real, L0_ffn_w_freq_imag, L0_ffn_bias), axis=-1)
    return x

_drawn_inputs = setup_inputs


def setup_inputs(seed=0):
    import zlib

    import numpy as np

    out = dict(_drawn_inputs(seed))
    spreads = {'L0_attn_bq': (0.0, 2.0),
     'L0_attn_bk': (0.0, 2.0),
     'L0_attn_bv': (0.0, 0.1),
     'L0_attn_bd': (0.0, 0.1),
     'L0_attn_gamma': (1.0, 0.2),
     'L0_attn_beta': (0.0, 0.1)}
    factors = {'L0_attn_Wq': 8.0, 'L0_attn_Wk': 8.0, 'L0_attn_Wv': 4.908, 'L0_ffn_bias': 21.837}
    for name, (base, spread) in spreads.items():
        noise = np.random.default_rng([zlib.crc32(name.encode()), seed]).standard_normal(out[name].shape)
        drawn = base * np.exp(spread * noise) if base else spread * noise
        out[name] = jnp.asarray(drawn.astype(out[name].dtype))
    for name, factor in factors.items():
        out[name] = (out[name] * factor).astype(out[name].dtype)
    return out
```

```python
from contextlib import ExitStack

import concourse.bass as bass
from concourse import mybir

P = 128
TPG = 4
F32 = mybir.dt.float32
F32R = mybir.dt.float32r
I32 = mybir.dt.int32
U32 = mybir.dt.uint32
ALU = mybir.AluOpType
ACT = mybir.ActivationFunctionType
EPS_LN = 1e-5
EPS_INNER = 1e-12
EPS_ATTN = 1e-6
RSQRT_MAGIC = 1597463007
NEWTON = 3


def ticks(i, c):
    return c * 4 + (i - 3)


def two_back(i, c):
    return c * 4 - 4 if i < 2 else c * 4 + (i - 5)


def wait(eng, sem, value):
    if isinstance(value, int) and value <= 0:
        return
    eng.wait_ge(sem, value)


def wait_apart(eng, sem, value, settled, least):
    if not isinstance(value, int):
        value = eng.snap(value)
        eng.wait_ge(settled, least)
    eng.wait_ge(sem, value)


def build(nc, x, wq, wk, wv, wd, bq, bk, bv, bd, gamma, beta, wr, wi, fbias, dft, consts, out):
    ROWS, D = x.shape
    C = D // P
    B = 8
    NG = ROWS // (B * P * TPG)
    GR = TPG * P
    assert C == 4 and NG == 4 and D == 512 and GR == 512

    with ExitStack() as ctx:
        def sb(name, shape, dt=F32):
            return ctx.enter_context(nc.sbuf_tensor(name, shape, dt))

        def sem(name):
            return ctx.enter_context(nc.semaphore(name))

        def sems(name):
            return [sem(f"{name}{i}") for i in range(TPG)]

        q_T = sb("q_T", [P, C, NG * GR])
        w_qT = sb("w_qT", [P, 2, C, D], F32R)
        w_kT = sb("w_kT", [P, 2, C, D], F32R)
        w_m = sb("w_m", [P, 2, C, D], F32R)
        w_vT = sb("w_vT", [P, C, D])
        w_dT = sb("w_dT", [P, C, D])
        kvw = sb("kvw", [P, 2, C, D], F32R)
        act_T = sb("act_T", [P, 2, C, GR], F32R)
        x3_T = sb("x3_T", [P, 2, 2, C, P], F32R)
        xa = sb("xa", [P, TPG, D])
        xb = sb("xb", [P, TPG, D])
        x1f = sb("x1f", [P, TPG, D])
        x2 = sb("x2", [P, TPG, D])
        work = sb("work", [P, 8, D])
        k_acc = sb("k_acc", [P, D])
        kv_T = sb("kv_T", [P, C, P])
        ksum_bd = sb("ksum_bd", [P, C, P])
        gamma_bc = sb("gamma_bc", [P, D])
        beta_bc = sb("beta_bc", [P, D])
        bd_bc = sb("bd_bc", [P, D])
        bk1_bc = sb("bk1_bc", [P, D])
        bv_bc = sb("bv_bc", [P, D])
        fb_row = sb("fb_row", [P, D], F32R)
        cst = sb("cst", [P, 3, P])
        ident, head_mask, ones = cst[:, 0, :], cst[:, 1, :], cst[:, 2, :]
        ones_r = sb("ones_r", [P, P], F32R)
        bq_col = sb("bq_col", [P, C])
        bq1_col = sb("bq1_col", [P, C])
        nbq_col = sb("nbq_col", [P, C])
        eps_col = sb("eps_col", [P, 3])
        stats = sb("stats", [P, TPG, 6])
        mv1 = sb("mv1", [P, TPG, 2])
        r1 = sb("r1", [P, TPG])
        nm1 = sb("nm1", [P, TPG])
        nr = sb("nr", [P, 3, TPG])
        r1_all = sb("r1_all", [P, NG * TPG])
        r1_g = sb("r1_g", [P, TPG])
        bn = sb("bn", [P, 3, 2, 6])
        mv = sb("mv", [P, 3, 2, 2])
        sd = sb("sd", [P, 4, 2])
        rs = sb("rs", [P, 4, 2])
        nm = sb("nm", [P, 3, 2])
        ssq = sb("ssq", [P, 2])

        k_hi, k_lo = kvw[:, 0, 0:2, :], kvw[:, 0, 2:4, :]
        x1_hi, x1_lo = kvw[:, 1, 0:2, :], kvw[:, 1, 2:4, :]
        k1, e_k, k_f, e_q = (work[:, 2 * j:2 * j + 2, :] for j in range(4))
        h, x3, qp = (work[:, 2 * j:2 * j + 2, :] for j in range(3))
        rec, junk = work[:, 6, :], work[:, 7, :]
        kx_T = work[:, 0:4, :]
        cosm, sinm, wr_sb, wi_sb = (q_T[:, j, :].rearrange("p (c n) -> p c n", c=C) for j in range(4))
        ncos = work[:, 0:4, :]
        p_T, r_T = xb, x2

        banks = [ctx.enter_context(nc.psum_tensor(f"bank{i}", [P, D], F32)) for i in range(8)]
        kx_ps = banks[0:4]
        hs_ps, den_ps = banks[0:2], banks[2:4]
        mm_ps = banks[4:6]
        t_ps = banks[6:8]

        w_in = sem("w_in"); w_in2 = sem("w_in2"); w_in3 = sem("w_in3"); split_hi = sem("split_hi"); split_done = sem("split_done")
        m1_ps = sem("m1_ps"); m1_act = sem("m1_act"); m1_dve = sem("m1_dve"); m2_ps = sem("m2_ps"); m2_c = sem("m2_c"); m2_hi = sem("m2_hi"); m2_out = sem("m2_out")
        pre = sem("pre"); setup_done = sem("setup_done")
        xa_in, xb_in, out_st = sems("xa_in"), sems("xb_in"), sems("out_st")
        x1f_ok, x1t_ps, x1lo_ok, k_ps, x2_ok = sems("x1f_ok"), sems("x1t_ps"), sems("x1lo_ok"), sems("k_ps"), sems("x2_ok")
        dve_ln1 = sem("dve_ln1"); ln1_bn = sem("ln1_bn"); ln1_ok = sem("ln1_ok")
        xthi, xtlo = sem("xthi"), sem("xtlo")
        q_ps, rq_ok, eq_ok, q_ok, rk_ok = sem("q_ps"), sem("rq_ok"), sem("eq_ok"), sem("q_ok"), sem("rk_ok")
        k1_ok, ek_ok, k_ok, khi_ok, klo_ok, kacc_ok = sem("k1_ok"), sem("ek_ok"), sem("k_ok"), sem("khi_ok"), sem("klo_ok"), sem("kacc_ok")
        kacc_zero = sem("kacc_zero")
        x1hi_ok, kx_done = sem("x1hi_ok"), sem("kx_done")
        ksum_ps, ksum_ok, kx_act, kx_dve, kv_ps, kv_ok = sem("ksum_ps"), sem("ksum_ok"), sem("kx_act"), sem("kx_dve"), sem("kv_ps"), sem("kv_ok")
        kvw_ps, kvwhi, kvwlo = sem("kvw_ps"), sem("kvwhi"), sem("kvwlo")
        d_ps, rec_ok, qp_ok, qhi_ok, qlo_ok = sem("d_ps"), sem("rec_ok"), sem("qp_ok"), sem("qhi_ok"), sem("qlo_ok")
        r1g_ok = sem("r1g_ok")
        hs_done, h_ok, bd_ok = sem("hs_done"), sem("h_ok"), sem("bd_ok")
        bn_ok = [sem(f"bn_ok{j}") for j in range(3)]
        mv_ok = [sem(f"mv_ok{j}") for j in range(3)]
        sd_ok = [sem(f"sd_ok{j}") for j in range(4)]
        rs_ok = [sem(f"rs_ok{j}") for j in range(4)]
        nm_ok = [sem(f"nm_ok{j}") for j in range(3)]
        n_ok, gam_ok, gb_ok, u_ok = sem("n_ok"), sem("gam_ok"), sem("gb_ok"), sem("u_ok")
        x3_ok, x3t_ps, x3hi, x3lo = sem("x3_ok"), sem("x3t_ps"), sem("x3hi"), sem("x3lo")
        y_ps, ysq_ok, fin_ok = sem("y_ps"), sem("ysq_ok"), sem("fin_ok")

        chunked = lambda a: a.rearrange("(c p) n -> p c n", p=P)
        block = ctx.enter_context(nc.Block())

        @block.sync
        def _(sp):
            def load_xa(i, c, first_row):
                wait(sp, x1f_ok[i], c - 1)
                sp.dma_start(xa[:, i, :], x[bass.ds(first_row + i * P, P), :]).then_inc(xa_in[i], 16)

            def load_xb(i, c, first_row):
                wait(sp, x2_ok[i], c - 1)
                sp.dma_start(xb[:, i, :], x[bass.ds(first_row + i * P, P), :]).then_inc(xb_in[i], 16)

            def store(i, c, first_row):
                wait(sp, fin_ok, ticks(i, c))
                sp.dma_start(out[bass.ds(first_row + i * P, P), :], x2[:, i, :]).then_inc(out_st[i], 16)

            for dst, src in ((wr_sb, chunked(wr)), (wi_sb, chunked(wi)), (cosm, chunked(dft[0])),
                             (sinm, chunked(dft[1])), (ncos, chunked(dft[2])), (cst[:], consts)):
                sp.dma_start(dst, src).then_inc(w_in, 16)
            for i in range(TPG):
                load_xa(i, 1, 0)
            for dst, src in ((gamma_bc[:], gamma), (beta_bc[:], beta), (bd_bc[:], bd), (bk1_bc[:], bk), (bv_bc[:], bv)):
                sp.dma_start(dst, src.partition_broadcast(P)).then_inc(w_in2, 16)
            sp.dma_start(bq_col[:], bq).then_inc(w_in2, 16)
            sp.dma_start(w_vT[:], chunked(wv)).then_inc(w_in2, 16)
            sp.dma_start(w_dT[:], chunked(wd)).then_inc(w_in2, 16)
            sp.dma_start(x1f[:], chunked(wq)).then_inc(w_in3, 16)
            sp.wait_ge(split_done, 1)
            sp.dma_start(x1f[:], chunked(wk)).then_inc(w_in3, 16)
            sp.wait_ge(split_done, 2)
            sp.dma_start(x1f[:, 0, :], fbias.partition_broadcast(P)).then_inc(w_in3, 16)
            sp.wait_ge(setup_done, 1)

            def batch(b, last):
                row = b * (NG * GR)
                for i in range(TPG):
                    load_xb(i, b * NG + 1, row)
                for g in range(NG):
                    wrapped = last and g == NG - 1
                    for i in range(TPG):
                        load_xa(i, b * NG + (g + 2), 0 if wrapped else row + (g + 1) * GR)
                for g in range(NG):
                    for i in range(TPG):
                        store(i, b * NG + (g + 1), row + g * GR)
                        if g + 1 < NG:
                            load_xb(i, b * NG + (g + 2), row + (g + 1) * GR)

            with sp.Fori(0, B - 1) as b:
                batch(b, False)
            batch(B - 1, True)
            for i in range(TPG):
                sp.wait_ge(out_st[i], 16 * B * NG)

        @block.gpsimd
        def _(pool):
            pool.memset(eps_col[:, 0:1], EPS_LN).then_inc(pre, 1)
            pool.memset(eps_col[:, 1:2], EPS_INNER).then_inc(pre, 1)
            pool.memset(eps_col[:, 2:3], 1.0).then_inc(pre, 1)

            def x1lo(i, c):
                pool.wait_ge(x1hi_ok, ticks(i, c))
                pool.tensor_tensor(x1_lo[:, i % 2, :], x1f[:, i, :], x1_hi[:, i % 2, :], ALU.subtract).then_inc(x1lo_ok[i], 1)

            def kacc(i, c, b):
                pool.wait_ge(k_ok, ticks(i, c))
                pool.wait_ge(kacc_zero, b + 1)
                if i:
                    pool.wait_ge(kacc_ok, ticks(i - 1, c))
                else:
                    wait(pool, kacc_ok, c * 4 - 4)
                pool.tensor_tensor(k_acc[:], k_acc[:], k_f[:, i % 2, :], ALU.add).then_inc(kacc_ok, 1)

            def add_bd(i, c):
                pool.wait_ge(h_ok, ticks(i, c))
                pool.tensor_tensor(h[:, i % 2, :], h[:, i % 2, :], bd_bc[:], ALU.add).then_inc(bd_ok, 1)

            def affine(i, c):
                pool.wait_ge(n_ok, ticks(i, c))
                pool.tensor_tensor(h[:, i % 2, :], h[:, i % 2, :], gamma_bc[:], ALU.mult).then_inc(gam_ok, 1)
                pool.wait_ge(gam_ok, ticks(i, c))
                pool.tensor_tensor(h[:, i % 2, :], h[:, i % 2, :], beta_bc[:], ALU.add).then_inc(gb_ok, 1)

            def qlo(u, c):
                pool.wait_ge(qhi_ok, ticks(u, c))
                pool.tensor_tensor(act_T[:, 1, u, :], qp[:, u % 2, :], act_T[:, 0, u, :], ALU.subtract).then_inc(qlo_ok, 1)

            with pool.Fori(0, B) as b:
                wait_apart(pool, kv_ps, b, pre, 3)
                pool.memset(k_acc[:], 0.0).then_inc(kacc_zero, 1)
                with pool.Fori(0, NG) as g:
                    c = pool.snap(b * NG + g + 1)
                    x1lo(0, c)
                    x1lo(1, c)
                    kacc(0, c, b)
                    kacc(1, c, b)
                    x1lo(2, c)
                    kacc(2, c, b)
                    x1lo(3, c)
                    kacc(3, c, b)
                c0 = pool.snap(b * NG + 1)
                for u in range(C):
                    qlo(u, c0)
                with pool.Fori(0, NG - 1) as g:
                    c = pool.snap(b * NG + g + 1)
                    for i in range(TPG):
                        add_bd(i, c)
                        affine(i, c)
                    for u in range(C):
                        qlo(u, c + 1)
                c3 = pool.snap(b * NG + NG)
                for i in range(TPG):
                    add_bd(i, c3)
                    affine(i, c3)

        @block.scalar
        def _(act):
            def copy(dst, src):
                return act.activation(dst, src, ACT.Copy)

            def make_x1f(i, c):
                act.wait_ge(ln1_ok, c)
                wait(act, x1t_ps[i], c - 1)
                wait(act, x1lo_ok[i], c - 1)
                act.activation(x1f[:, i, :], xa[:, i, :], ACT.Identity, bias=nm1[:, i:i + 1], scale=r1[:, i:i + 1]).then_inc(x1f_ok[i], 1)

            def xt_hi(i, c):
                act.wait_ge(x1t_ps[i], c)
                wait(act, k_ps[i], c - 1)
                copy(act_T[:, 0, :, i * P:(i + 1) * P], t_ps[i % 2][:].rearrange("p (c n) -> p c n", c=C)).then_inc(xthi, 1)

            def exp_q(u, c):
                act.wait_ge(q_ps, ticks(u, c))
                wait(act, q_ok, two_back(u, c))
                act.activation(e_q[:, u % 2, :], mm_ps[u % 2][:], ACT.Relu, bias=nbq_col[:, u:u + 1], scale=-1.0).then_inc(rq_ok, 1)
                act.wait_ge(rq_ok, ticks(u, c))
                act.activation(e_q[:, u % 2, :], e_q[:, u % 2, :], ACT.Exp, scale=-1.0).then_inc(eq_ok, 1)

            def split_x1(i, c, b):
                wait(act, kx_done, two_back(i, c))
                wait(act, hs_done, b * (NG * TPG))
                wait(act, x1f_ok[i], c)
                copy(x1_hi[:, i % 2, :], x1f[:, i, :]).then_inc(x1hi_ok, 1)

            def exp_k(i, c):
                act.wait_ge(k1_ok, ticks(i, c))
                wait(act, k_ok, two_back(i, c))
                act.activation(e_k[:, i % 2, :], k1[:, i % 2, :], ACT.Relu, bias=eps_col[:, 2:3], scale=-1.0).then_inc(rk_ok, 1)
                act.wait_ge(rk_ok, ticks(i, c))
                act.activation(e_k[:, i % 2, :], e_k[:, i % 2, :], ACT.Exp, scale=-1.0).then_inc(ek_ok, 1)

            def split_k(i, c):
                act.wait_ge(k_ok, ticks(i, c))
                wait(act, kx_done, two_back(i, c))
                copy(k_hi[:, i % 2, :], k_f[:, i % 2, :]).then_inc(khi_ok, 1)

            def q_hi(u, c):
                act.wait_ge(qp_ok, ticks(u, c))
                wait(act, hs_done, c * 4 - 4)
                copy(act_T[:, 0, u, :], qp[:, u % 2, :]).then_inc(qhi_ok, 1)

            def root(j, i, c, eps):
                act.wait_ge(mv_ok[j], ticks(i, c))
                act.activation(sd[:, j, i % 2:i % 2 + 1], mv[:, j, i % 2, 1:2], ACT.Sqrt, bias=eps_col[:, eps:eps + 1]).then_inc(sd_ok[j], 1)

            def normalise(j, i, c, dst, src, done):
                act.wait_ge(nm_ok[j], ticks(i, c))
                act.activation(dst, src, ACT.Identity, bias=nm[:, j, i % 2:i % 2 + 1], scale=rs[:, j, i % 2:i % 2 + 1]).then_inc(done, 1)

            def make_x3(i, c):
                wait(act, x3t_ps, two_back(i, c))
                normalise(2, i, c, x3[:, i % 2, :], x2[:, i, :], x3_ok)

            def x3_hi(i, c):
                act.wait_ge(x3t_ps, ticks(i, c))
                wait(act, y_ps, two_back(i, c))
                copy(x3_T[:, i % 2, 0, :, :], t_ps[i % 2][:].rearrange("p (c n) -> p c n", c=C)).then_inc(x3hi, 1)

            def y_root(i, c):
                act.wait_ge(y_ps, ticks(i, c))
                act.activation(junk, mm_ps[i % 2][:], ACT.Square, accum_out=ssq[:, i % 2:i % 2 + 1]).then_inc(ysq_ok, 1)
                act.wait_ge(ysq_ok, ticks(i, c))
                act.activation(sd[:, 3, i % 2:i % 2 + 1], ssq[:, i % 2:i % 2 + 1], ACT.Sqrt, bias=eps_col[:, 0:1], scale=1.0 / D).then_inc(sd_ok[3], 1)

            act.wait_ge(pre, 3)
            for n, w in enumerate((w_qT, w_kT)):
                act.wait_ge(w_in3, 16 * (n + 1))
                copy(w[:, 0], x1f[:]).then_inc(split_hi, 1)
            for n in range(C):
                act.wait_ge(m1_ps, 2 * n + 1)
                copy(p_T[:, n, :], banks[0 + 2 * (n % 2)][:]).then_inc(m1_act, 1)
            for n in range(C):
                act.wait_ge(m2_c, n + 1)
                copy(w_m[:, 0, n, :], work[:, 4 + n, :]).then_inc(m2_hi, 1)
            act.wait_ge(setup_done, 1)
            for i in range(TPG):
                make_x1f(i, 1)
            for i in range(TPG):
                xt_hi(i, 1)

            def phase1(c, b, more):
                exp_q(0, c)
                split_x1(0, c, b)
                exp_q(1, c)
                split_x1(1, c, b)
                exp_q(2, c)
                exp_q(3, c)
                make_x1f(0, c + 1)
                exp_k(0, c)
                make_x1f(1, c + 1)
                split_k(0, c)
                if more:
                    xt_hi(0, c + 1)
                exp_k(1, c)
                split_k(1, c)
                if more:
                    xt_hi(1, c + 1)
                split_x1(2, c, b)
                make_x1f(2, c + 1)
                exp_k(2, c)
                split_k(2, c)
                split_x1(3, c, b)
                make_x1f(3, c + 1)
                if more:
                    xt_hi(2, c + 1)
                exp_k(3, c)
                split_k(3, c)
                if more:
                    xt_hi(3, c + 1)

            def slot(i, c, here, before, y, t):
                if before:
                    j, cj = (i - 1, c) if i else (TPG - 1, c - 1)
                    root(1, j, cj, 0)
                if here:
                    root(0, i, c, 1)
                if before:
                    normalise(1, j, cj, h[:, j % 2, :], h[:, j % 2, :], u_ok)
                if here:
                    normalise(0, i, c, h[:, i % 2, :], h[:, i % 2, :], n_ok)
                if y is not None:
                    y_root(*y)
                if before:
                    root(2, j, cj, 0)
                    make_x3(j, cj)
                if t is not None:
                    x3_hi(*t)

            def phase2(c, prev, more):
                slot(0, c, True, prev, (1, c - 1) if prev else None, (2, c - 1) if prev else None)
                slot(1, c, True, True, (2, c - 1) if prev else None, (3, c - 1) if prev else None)
                slot(2, c, True, True, (3, c - 1) if prev else None, None)
                slot(3, c, True, True, None, (0, c))
                if more:
                    for u in range(C):
                        q_hi(u, c + 1)
                y_root(0, c)
                x3_hi(1, c)

            with act.Fori(0, B) as b:
                with act.Fori(0, NG - 1) as g:
                    phase1(act.snap(b * NG + g + 1), b, True)
                c3 = act.snap(b * NG + NG)
                phase1(c3, b, False)
                act.wait_ge(kx_done, c3 * 4)
                for j in (0, 2):
                    copy(kx_T[:, j, :], kx_ps[j][:]).then_inc(kx_act, 1)
                for u in range(C):
                    act.wait_ge(kvw_ps, b * C + (u + 1))
                    copy(kvw[:, 0, u, :], banks[u][:]).then_inc(kvwhi, 1)
                c0 = act.snap(b * NG + 1)
                for u in range(C):
                    q_hi(u, c0)
                phase2(c0, False, True)
                with act.Fori(1, NG - 1) as g:
                    phase2(act.snap(b * NG + g + 1), True, True)
                c3 = act.snap(b * NG + NG)
                phase2(c3, True, False)
                slot(0, c3 + 1, False, True, (1, c3), (2, c3))
                y_root(2, c3)
                x3_hi(3, c3)
                y_root(3, c3)
                for i in range(TPG):
                    xt_hi(i, c3 + 1)

        @block.vector
        def _(dve):
            dve.wait_ge(w_in2, 16 * 8)
            dve.tensor_scalar(bk1_bc[:], bk1_bc[:], 1.0, None, ALU.add)
            dve.tensor_scalar(bq1_col[:], bq_col[:], 1.0, None, ALU.add)
            dve.tensor_scalar(nbq_col[:], bq_col[:], -1.0, None, ALU.mult)
            dve.wait_ge(w_in, 16 * 6)
            dve.tensor_copy(ones_r[:], ones)
            for n, w in enumerate((w_qT, w_kT)):
                dve.wait_ge(split_hi, n + 1)
                dve.tensor_tensor(w[:, 1], x1f[:], w[:, 0], ALU.subtract).then_inc(split_done, 1)
            for n in range(C):
                dve.wait_ge(m1_ps, 2 * n + 2)
                dve.tensor_copy(r_T[:, n, :], banks[1 + 2 * (n % 2)][:]).then_inc(m1_dve, 1)
            setup_steps = [0]

            def link(ins):
                setup_steps[0] += 1
                ins.then_inc(m2_out, 1)
                dve.wait_ge(m2_out, setup_steps[0])

            def centre(dst, src, scale):
                link(dve.bn_stats(bn[:, 0, 0, :], src))
                link(dve.bn_aggr(mv[:, 0, 0, :], bn[:, 0, 0, :]))
                return dve.tensor_scalar(dst, src, mv[:, 0, 0, 0:1], scale, ALU.subtract, ALU.mult)

            for n in range(C):
                dve.wait_ge(m2_ps, n + 1)
                centre(work[:, 4 + n, :], banks[4 + n % 2][:], 1.0 / D).then_inc(m2_c, 1)
                dve.wait_ge(m2_hi, n + 1)
                link(dve.tensor_tensor(w_m[:, 1, n, :], work[:, 4 + n, :], w_m[:, 0, n, :], ALU.subtract))
            dve.wait_ge(w_in3, 16 * 3)
            link(centre(x1f[:, 1, :], x1f[:, 0, :], 1.0))
            link(dve.tensor_copy(fb_row[:], x1f[:, 1, :]))
            link(dve.tensor_tensor(x1f[:, 2, :], x1f[:, 1, :], fb_row[:], ALU.subtract))
            link(dve.tensor_scalar(x1f[:, 3, :], x1f[:, 2, :], ident[:, 1:2], None, ALU.mult))
            link(dve.tensor_copy(x1f[:, 0, :], fb_row[:]))
            dve.scalar_tensor_tensor(out=fb_row[:], in0=x1f[:, 0, :], scalar=ident[:, 0:1], in1=x1f[:, 3, :],
                                     op0=ALU.mult, op1=ALU.add).then_inc(setup_done, 1)

            def ln1_stats(i, c):
                dve.wait_ge(xa_in[i], c * 16)
                dve.bn_stats(stats[:, i, :], xa[:, i, :]).then_inc(ln1_bn, 1)

            LN1_STEPS = 2 + 3 * NEWTON + 2

            def ln1_finish(c, g=None):
                n = [0]

                def step(ins):
                    n[0] += 1
                    ins.then_inc(dve_ln1, 1)
                    dve.wait_ge(dve_ln1, (c - 1) * LN1_STEPS + n[0])

                dve.wait_ge(ln1_bn, c * 4)
                if g is not None:
                    dve.tensor_copy(r1_all[:, bass.ds(g * TPG, TPG)], r1[:])
                for i in range(TPG):
                    ins = dve.bn_aggr(mv1[:, i, :], stats[:, i, :])
                step(ins)
                v, y, a = nr[:, 0, :], nr[:, 1, :], nr[:, 2, :]
                step(dve.tensor_scalar(v, mv1[:, :, 1], EPS_LN, None, ALU.add))
                step(dve.tensor_scalar(a.bitcast(U32), v.bitcast(U32), 1, None, ALU.logical_shift_right))
                wait(dve, x1f_ok[3], c - 1)
                step(dve.tensor_scalar(y.bitcast(I32), a.bitcast(I32), -1, RSQRT_MAGIC, ALU.mult, ALU.add))
                for s in range(NEWTON):
                    step(dve.scalar_tensor_tensor(out=a, in0=y, scalar=-0.5, in1=v, op0=ALU.mult, op1=ALU.mult))
                    step(dve.tensor_tensor(a, a, y, ALU.mult))
                    last = s == NEWTON - 1
                    step(dve.scalar_tensor_tensor(out=r1[:] if last else y, in0=a, scalar=1.5, in1=y, op0=ALU.add, op1=ALU.mult))
                assert n[0] == LN1_STEPS
                dve.scalar_tensor_tensor(out=nm1[:], in0=mv1[:, :, 0], scalar=-1.0, in1=r1[:], op0=ALU.mult,
                                         op1=ALU.mult).then_inc(ln1_ok, 1)

            def xt_lo(i, c):
                dve.wait_ge(xthi, ticks(i, c))
                s = slice(i * P, (i + 1) * P)
                dve.tensor_tensor(act_T[:, 1, :, s], t_ps[i % 2][:].rearrange("p (c n) -> p c n", c=C),
                                  act_T[:, 0, :, s], ALU.subtract).then_inc(xtlo, 1)

            def q_feature(u, c, g):
                dve.wait_ge(eq_ok, ticks(u, c))
                dve.scalar_tensor_tensor(out=q_T[:, u, bass.ds(g * GR, GR)], in0=mm_ps[u % 2][:], scalar=bq1_col[:, u:u + 1],
                                         in1=e_q[:, u % 2, :], op0=ALU.add, op1=ALU.max).then_inc(q_ok, 1)

            def k_bias(i, c):
                dve.wait_ge(k_ps[i], c)
                wait(dve, ek_ok, two_back(i, c))
                dve.tensor_tensor(k1[:, i % 2, :], mm_ps[i % 2][:], bk1_bc[:], ALU.add).then_inc(k1_ok, 1)

            def k_feature(i, c):
                dve.wait_ge(ek_ok, ticks(i, c))
                wait(dve, kacc_ok, two_back(i, c))
                wait(dve, khi_ok, two_back(i, c))
                dve.tensor_tensor(k_f[:, i % 2, :], e_k[:, i % 2, :], k1[:, i % 2, :], ALU.max).then_inc(k_ok, 1)

            def k_low(i, c):
                dve.wait_ge(khi_ok, ticks(i, c))
                dve.tensor_tensor(k_lo[:, i % 2, :], k_f[:, i % 2, :], k_hi[:, i % 2, :], ALU.subtract).then_inc(klo_ok, 1)

            def phase1(c, g, more):
                for u in range(C):
                    q_feature(u, c, g)
                    ln1_stats(u, c + 1)
                ln1_finish(c + 1, g)
                for i in range(TPG):
                    k_bias(i, c)
                    k_feature(i, c)
                    k_low(i, c)
                    if more:
                        xt_lo(i, c + 1)

            def q_scaled(u, c, g):
                dve.wait_ge(d_ps, ticks(u, c))
                wait(dve, qp_ok, c * 4 + (u - 4))
                dve.reciprocal(rec, den_ps[u % 2][:]).then_inc(rec_ok, 1)
                dve.wait_ge(rec_ok, ticks(u, c))
                wait(dve, qlo_ok, two_back(u, c))
                dve.tensor_tensor(qp[:, u % 2, :], rec, q_T[:, u, bass.ds(g * GR, GR)], ALU.mult).then_inc(qp_ok, 1)

            def residual(i, c):
                dve.wait_ge(hs_done, ticks(i, c))
                dve.wait_ge(xb_in[i], c * 16)
                dve.wait_ge(r1g_ok, c)
                dve.scalar_tensor_tensor(out=h[:, i % 2, :], in0=xb[:, i, :], scalar=r1_g[:, i:i + 1], in1=hs_ps[i % 2][:],
                                         op0=ALU.mult, op1=ALU.add).then_inc(h_ok, 1)

            def moments(j, i, c, src):
                dve.bn_stats(bn[:, j, i % 2, :], src).then_inc(bn_ok[j], 1)
                wait_apart(dve, bn_ok[j], ticks(i, c), pre, 3)
                dve.bn_aggr(mv[:, j, i % 2, :], bn[:, j, i % 2, :]).then_inc(mv_ok[j], 1)

            def scales(j, i, c):
                dve.wait_ge(sd_ok[j], ticks(i, c))
                dve.reciprocal(rs[:, j, i % 2:i % 2 + 1], sd[:, j, i % 2:i % 2 + 1]).then_inc(rs_ok[j], 1)
                dve.wait_ge(rs_ok[j], ticks(i, c))
                dve.scalar_tensor_tensor(out=nm[:, j, i % 2:i % 2 + 1], in0=mv[:, j, i % 2, 0:1], scalar=-1.0,
                                         in1=rs[:, j, i % 2:i % 2 + 1], op0=ALU.mult, op1=ALU.mult).then_inc(nm_ok[j], 1)

            def add_x(i, c):
                dve.wait_ge(u_ok, ticks(i, c))
                wait(dve, out_st[i], c * 16 - 16)
                dve.tensor_tensor(x2[:, i, :], xb[:, i, :], h[:, i % 2, :], ALU.add).then_inc(x2_ok[i], 1)
                dve.wait_ge(x2_ok[i], c)

            def x3_low(i, c):
                dve.wait_ge(x3hi, ticks(i, c))
                dve.tensor_tensor(x3_T[:, i % 2, 1, :, :], t_ps[i % 2][:].rearrange("p (c n) -> p c n", c=C),
                                  x3_T[:, i % 2, 0, :, :], ALU.subtract).then_inc(x3lo, 1)

            def finish(i, c):
                dve.wait_ge(sd_ok[3], ticks(i, c))
                dve.reciprocal(rs[:, 3, i % 2:i % 2 + 1], sd[:, 3, i % 2:i % 2 + 1]).then_inc(rs_ok[3], 1)
                dve.wait_ge(rs_ok[3], ticks(i, c))
                dve.scalar_tensor_tensor(out=x2[:, i, :], in0=mm_ps[i % 2][:], scalar=rs[:, 3, i % 2:i % 2 + 1],
                                         in1=x2[:, i, :], op0=ALU.mult, op1=ALU.add).then_inc(fin_ok, 1)

            def slot(i, c, here, before, y, t):
                if here:
                    residual(i, c)
                if before:
                    j, cj = (i - 1, c) if i else (TPG - 1, c - 1)
                    dve.wait_ge(gb_ok, ticks(j, cj))
                    moments(1, j, cj, h[:, j % 2, :])
                if here:
                    dve.wait_ge(bd_ok, ticks(i, c))
                    moments(0, i, c, h[:, i % 2, :])
                if before:
                    scales(1, j, cj)
                if here:
                    scales(0, i, c)
                if before:
                    add_x(j, cj)
                    moments(2, j, cj, x2[:, j, :])
                if y is not None:
                    finish(*y)
                if before:
                    scales(2, j, cj)
                if t is not None:
                    x3_low(*t)

            def phase2(c, g, prev, more):
                dve.tensor_copy(r1_g[:], r1_all[:, bass.ds(g * TPG, TPG)]).then_inc(r1g_ok, 1)
                slot(0, c, True, prev, (1, c - 1) if prev else None, (2, c - 1) if prev else None)
                slot(1, c, True, True, (2, c - 1) if prev else None, (3, c - 1) if prev else None)
                slot(2, c, True, True, (3, c - 1) if prev else None, None)
                slot(3, c, True, True, None, (0, c))
                if more:
                    for u in range(C):
                        q_scaled(u, c + 1, g + 1)
                finish(0, c)
                x3_low(1, c)

            for i in range(TPG):
                ln1_stats(i, 1)
            ln1_finish(1)
            for i in range(TPG):
                xt_lo(i, 1)

            with dve.Fori(0, B) as b:
                with dve.Fori(0, NG - 1) as g:
                    phase1(dve.snap(b * NG + g + 1), g, True)
                c3 = dve.snap(b * NG + NG)
                phase1(c3, NG - 1, False)
                dve.wait_ge(kx_done, c3 * 4)
                for j in (1, 3):
                    dve.tensor_copy(kx_T[:, j, :], kx_ps[j][:]).then_inc(kx_dve, 1)
                mask4 = head_mask.unsqueeze(1).broadcast_to([P, C, P])
                dve.wait_ge(ksum_ps, b + 1)
                dve.scalar_tensor_tensor(out=ksum_bd[:], in0=t_ps[1][:].rearrange("p (c n) -> p c n", c=C), scalar=EPS_ATTN,
                                         in1=mask4, op0=ALU.add, op1=ALU.mult).then_inc(ksum_ok, 1)
                dve.wait_ge(kv_ps, b + 1)
                dve.tensor_tensor(kv_T[:], t_ps[0][:].rearrange("p (c n) -> p c n", c=C), mask4, ALU.mult).then_inc(kv_ok, 1)
                for u in range(C):
                    dve.wait_ge(kvwhi, b * C + (u + 1))
                    dve.tensor_tensor(kvw[:, 1, u, :], banks[u][:], kvw[:, 0, u, :], ALU.subtract).then_inc(kvwlo, 1)
                c0 = dve.snap(b * NG + 1)
                for u in range(C):
                    q_scaled(u, c0, 0)
                phase2(c0, 0, False, True)
                with dve.Fori(1, NG - 1) as g:
                    phase2(dve.snap(b * NG + g + 1), g, True, True)
                c3 = dve.snap(b * NG + NG)
                phase2(c3, NG - 1, True, False)
                slot(0, c3 + 1, False, True, (1, c3), (2, c3))
                finish(2, c3)
                x3_low(3, c3)
                finish(3, c3)
                for i in range(TPG):
                    xt_lo(i, c3 + 1)

        @block.tensor
        def _(pe):
            def split_product(dst, left_hi, left_lo, right_hi, right_lo, start, stop, **kw):
                pe.matmul(dst, left_hi, right_hi, start=start, stop=False, **kw)
                pe.matmul(dst, left_hi, right_lo, start=False, stop=False, **kw)
                return pe.matmul(dst, left_lo, right_hi, start=False, stop=stop, **kw)

            pe.wait_ge(w_in, 16 * 6)
            for n in range(C):
                o = slice(n * P, (n + 1) * P)
                if n >= 2:
                    pe.wait_ge(m1_act, n - 1)
                    pe.wait_ge(m1_dve, n - 1)
                for bank, right_r, right_i in ((banks[2 * (n % 2)], cosm, sinm), (banks[2 * (n % 2) + 1], sinm, ncos)):
                    for j in range(C):
                        pe.matmul(bank[:], wr_sb[:, j, o], right_r[:, j, :], start=(j == 0), stop=False)
                        mm = pe.matmul(bank[:], wi_sb[:, j, o], right_i[:, j, :], start=False, stop=(j == C - 1))
                    mm.then_inc(m1_ps, 1)
            pe.wait_ge(m1_act, C)
            pe.wait_ge(m1_dve, C)
            for n in range(C):
                o = slice(n * P, (n + 1) * P)
                if n >= 2:
                    pe.wait_ge(m2_c, n - 1)
                for j in range(C):
                    pe.matmul(banks[4 + n % 2][:], p_T[:, j, o], cosm[:, j, :], start=(j == 0), stop=False)
                    mm = pe.matmul(banks[4 + n % 2][:], r_T[:, j, o], sinm[:, j, :], start=False, stop=(j == C - 1))
                mm.then_inc(m2_ps, 1)

            def transpose_x1(i, c):
                pe.wait_ge(x1f_ok[i], c)
                wait(pe, xtlo, two_back(i, c))
                for j in range(C):
                    mm = pe.transpose(t_ps[i % 2][:, j * P:(j + 1) * P], x1f[:, i, j * P:(j + 1) * P], ident)
                mm.then_inc(x1t_ps[i], 1)

            def project_q(u, c, b):
                wait(pe, xtlo, c * 4)
                if u < 2:
                    wait(pe, k1_ok, c * 4 - 4)
                    wait(pe, fin_ok, b * (NG * TPG))
                else:
                    pe.wait_ge(q_ok, ticks(u - 2, c))
                for j in range(C):
                    o = slice(u * P, (u + 1) * P)
                    mm = split_product(mm_ps[u % 2][:], w_qT[:, 0, j, o], w_qT[:, 1, j, o], act_T[:, 0, j, :], act_T[:, 1, j, :],
                                       j == 0, j == C - 1)
                mm.then_inc(q_ps, 1)

            def project_k(i, c):
                if i < 2:
                    pe.wait_ge(q_ok, ticks(i + 2, c))
                else:
                    pe.wait_ge(k1_ok, ticks(i - 2, c))
                for j in range(C):
                    s = slice(i * P, (i + 1) * P)
                    mm = split_product(mm_ps[i % 2][:], act_T[:, 0, j, s], act_T[:, 1, j, s], w_kT[:, 0, j, :], w_kT[:, 1, j, :],
                                       j == 0, j == C - 1)
                mm.then_inc(k_ps[i], 1)

            def outer_kx(i, c, first):
                pe.wait_ge(x1lo_ok[i], c)
                pe.wait_ge(klo_ok, ticks(i, c))
                for j in range(C):
                    o = slice(j * P, (j + 1) * P)
                    mm = split_product(kx_ps[j][:], x1_hi[:, i % 2, o], x1_lo[:, i % 2, o], k_hi[:, i % 2, :], k_lo[:, i % 2, :],
                                       first, False, skip_group_check=True)
                mm.then_inc(kx_done, 1)

            def phase1(c, b, first, more):
                for u in range(C):
                    project_q(u, c, b)
                project_k(0, c)
                if more:
                    transpose_x1(0, c + 1)
                project_k(1, c)
                if more:
                    transpose_x1(1, c + 1)
                outer_kx(0, c, first)
                project_k(2, c)
                outer_kx(1, c, False)
                if more:
                    transpose_x1(2, c + 1)
                project_k(3, c)
                outer_kx(2, c, False)
                if more:
                    transpose_x1(3, c + 1)
                outer_kx(3, c, False)

            def denominator(u, c, g):
                if u >= 2:
                    pe.wait_ge(rec_ok, ticks(u - 2, c))
                else:
                    wait(pe, rec_ok, c * 4 - 4)
                pe.matmul(den_ps[u % 2][:], ksum_bd[:, u, :], q_T[:, u, bass.ds(g * GR, GR)], start=True, stop=True).then_inc(d_ps, 1)

            def attention(i, c):
                wait(pe, qlo_ok, c * 4)
                wait(pe, h_ok, two_back(i, c))
                for u in range(C):
                    s = slice(i * P, (i + 1) * P)
                    mm = split_product(hs_ps[i % 2][:], act_T[:, 0, u, s], act_T[:, 1, u, s], kvw[:, 0, u, :], kvw[:, 1, u, :],
                                       u == 0, u == C - 1)
                mm.then_inc(hs_done, 1)

            def transpose_x3(i, c):
                pe.wait_ge(x3_ok, ticks(i, c))
                wait(pe, x3lo, two_back(i, c))
                for j in range(C):
                    mm = pe.transpose(t_ps[i % 2][:, j * P:(j + 1) * P], x3[:, i % 2, j * P:(j + 1) * P], ident)
                mm.then_inc(x3t_ps, 1)

            def ffn(i, c):
                pe.wait_ge(x3lo, ticks(i, c))
                wait(pe, fin_ok, two_back(i, c))
                pe.matmul(mm_ps[i % 2][:], ones_r[:], fb_row[:], start=True, stop=False)
                for j in range(C):
                    mm = split_product(mm_ps[i % 2][:], x3_T[:, i % 2, 0, j, :], x3_T[:, i % 2, 1, j, :], w_m[:, 0, j, :], w_m[:, 1, j, :],
                                       False, j == C - 1)
                mm.then_inc(y_ps, 1)

            def phase2(c, g, prev, more):
                attention(0, c)
                if prev:
                    ffn(1, c - 1)
                    transpose_x3(2, c - 1)
                attention(1, c)
                if prev:
                    ffn(2, c - 1)
                    transpose_x3(3, c - 1)
                attention(2, c)
                if prev:
                    ffn(3, c - 1)
                attention(3, c)
                transpose_x3(0, c)
                if more:
                    for u in range(C):
                        denominator(u, c + 1, g + 1)
                ffn(0, c)
                transpose_x3(1, c)

            pe.wait_ge(setup_done, 1)
            for i in range(TPG):
                transpose_x1(i, 1)

            with pe.Fori(0, B) as b:
                pe.wait_ge(h_ok, b * (NG * TPG))
                pe.wait_ge(rec_ok, b * (NG * TPG))
                phase1(pe.snap(b * NG + 1), b, True, True)
                with pe.Fori(1, NG - 1) as g:
                    phase1(pe.snap(b * NG + g + 1), b, False, True)
                c3 = pe.snap(b * NG + NG)
                phase1(c3, b, False, False)

                pe.wait_ge(kacc_ok, c3 * 4)
                wait(pe, xtlo, c3 * 4)
                for u in range(C):
                    mm = pe.matmul(t_ps[1][:, u * P:(u + 1) * P], k_acc[:, u * P:(u + 1) * P], ones, start=True, stop=True)
                mm.then_inc(ksum_ps, 1)
                pe.wait_ge(kx_act, b * 2 + 2)
                pe.wait_ge(kx_dve, b * 2 + 2)
                for u in range(C):
                    o = slice(u * P, (u + 1) * P)
                    for j in range(C):
                        pe.matmul(t_ps[0][:, o], w_vT[:, j, o], kx_T[:, j, o], start=(j == 0), stop=False)
                    mm = pe.matmul(t_ps[0][:, o], bv_bc[:, o], k_acc[:, o], start=False, stop=True)
                mm.then_inc(kv_ps, 1)
                pe.wait_ge(kv_ok, b + 1)
                for u in range(C):
                    pe.matmul(banks[u][:], kv_T[:, u, :], w_dT[:, u, :], start=True, stop=True).then_inc(kvw_ps, 1)
                pe.wait_ge(ksum_ok, b + 1)
                pe.wait_ge(kvwlo, b * C + C)
                c0 = pe.snap(b * NG + 1)
                for u in range(C):
                    denominator(u, c0, 0)

                phase2(c0, 0, False, True)
                with pe.Fori(1, NG - 1) as g:
                    phase2(pe.snap(b * NG + g + 1), g, True, True)
                c3 = pe.snap(b * NG + NG)
                phase2(c3, NG - 1, True, False)
                ffn(1, c3)
                transpose_x3(2, c3)
                ffn(2, c3)
                transpose_x3(3, c3)
                ffn(3, c3)
                pe.wait_ge(x3lo, c3 * 4)
                for i in range(TPG):
                    transpose_x1(i, c3 + 1)


def constants():
    import numpy as np
    d = 512
    jk = np.outer(np.arange(d), np.arange(d)) % d
    cos, sin = np.cos(2 * np.pi * jk / d), np.sin(2 * np.pi * jk / d)
    dft = np.stack([cos, sin, -cos]).astype(np.float32)
    head = np.arange(P) // 32
    consts = np.stack([np.eye(P), head[:, None] == head[None, :], np.ones((P, P))], axis=1).astype(np.float32)
    return dft, np.ascontiguousarray(consts)


def kernel(**inputs):
    import numpy as np
    import concourse.bacc as bacc
    from concourse.bass_utils import run_bass_kernel_spmd

    a = {k[3:]: np.asarray(v) for k, v in inputs.items()}
    x = np.ascontiguousarray(a["attn_input_tensor"]).reshape(-1, 512)
    dft, consts = constants()
    arrays = {"x": x}
    for n, key in (("wq", "attn_Wq"), ("wk", "attn_Wk"), ("wv", "attn_Wv"), ("wd", "attn_Wd")):
        arrays[n] = np.ascontiguousarray(a[key].T)
    arrays["bq"] = np.ascontiguousarray(a["attn_bq"].reshape(4, P).T)
    for n, key in (("bk", "attn_bk"), ("bv", "attn_bv"), ("bd", "attn_bd"), ("gamma", "attn_gamma"), ("beta", "attn_beta"),
                   ("wr", "ffn_w_freq_real"), ("wi", "ffn_w_freq_imag"), ("fbias", "ffn_bias")):
        arrays[n] = np.ascontiguousarray(a[key])
    arrays["dft"], arrays["consts"] = dft, consts

    nc = bacc.Bacc("TRN2", target_bir_lowering=False, num_devices=1)
    aps = {n: nc.dram_tensor(f"{n}_dram", v.shape, F32, kind="ExternalInput").ap() for n, v in arrays.items()}
    out = nc.dram_tensor("out_dram", x.shape, F32, kind="ExternalOutput").ap()
    build(nc, out=out, **aps)
    r = run_bass_kernel_spmd(nc, [{f"{n}_dram": v for n, v in arrays.items()}], core_ids=[0])
    return r.results[0]["out_dram"].reshape(8, 2048, 512)
```

```python
from contextlib import ExitStack

import concourse.bass as bass
from concourse import mybir

P = 128
TPG = 4
F32 = mybir.dt.float32
F32R = mybir.dt.float32r
I32 = mybir.dt.int32
U32 = mybir.dt.uint32
ALU = mybir.AluOpType
ACT = mybir.ActivationFunctionType
EPS_LN = 1e-5
EPS_INNER = 1e-12
EPS_ATTN = 1e-6
RSQRT_MAGIC = 1597463007
NEWTON = 3


def ticks(i, c):
    return c * 4 + (i - 3)


def two_back(i, c):
    return c * 4 - 4 if i < 2 else c * 4 + (i - 5)


def wait(eng, sem, count):
    if isinstance(count, int) and count <= 0:
        return
    eng.wait_ge(sem, count + 1)


def wait_apart(eng, sem, value, settled, least):
    eng.wait_ge(settled, least)
    eng.wait_ge(sem, value + 1)


def build(nc, x, wq, wk, wv, wd, bq, bk, bv, bd, gamma, beta, wr, wi, fbias, dft, consts, spread_f, out):
    ROWS, D = x.shape
    C = D // P
    B = 8
    NG = ROWS // (B * P * TPG)
    NH = 16
    GR = TPG * P
    assert C == 4 and NG == 4 and D == 512 and GR == 512

    with ExitStack() as ctx:
        def sb(name, shape, dt=F32):
            return ctx.enter_context(nc.sbuf_tensor(name, shape, dt))

        def sem(name):
            return ctx.enter_context(nc.semaphore(name))

        def sems(name):
            return [sem(f"{name}{i}") for i in range(TPG)]

        q_T = sb("q_T", [P, C, NG * GR])
        w_qT = sb("w_qT", [P, 2, C, D], F32R)
        w_kT = sb("w_kT", [P, 2, C, D], F32R)
        w_m = sb("w_m", [P, 2, C, D], F32R)
        w_vT = sb("w_vT", [P, C, D])
        w_dT = sb("w_dT", [P, C, D])
        kvw = sb("kvw", [P, 2, C, D], F32R)
        act_T = sb("act_T", [P, 2, C, GR], F32R)
        x3_T = sb("x3_T", [P, 2, 2, C, P], F32R)
        xa = sb("xa", [P, TPG, D])
        xb = sb("xb", [P, TPG, D])
        x1f = sb("x1f", [P, TPG, D])
        x2 = sb("x2", [P, TPG, D])
        work = sb("work", [P, 8, D])
        k_acc = sb("k_acc", [P, D])
        kv_T = sb("kv_T", [P, C, P])
        ksum_h = sb("ksum_h", [P, C, NH])
        z_hl = sb("z_hl", [NH, 2, GR], F32R)
        gamma_bc = sb("gamma_bc", [P, D])
        beta_bc = sb("beta_bc", [P, D])
        bk1_bc = sb("bk1_bc", [P, D])
        bv_bc = sb("bv_bc", [P, D])
        bias_rows = sb("bias_rows", [P, D], F32R)
        cst = sb("cst", [P, 3 * P + C * NH])
        ident, head_mask, ones = cst[:, 0:P], cst[:, P:2 * P], cst[:, 2 * P:3 * P]
        own_head = cst[:, 3 * P:].rearrange("p (u h) -> p u h", h=NH)
        spread = sb("spread", [NH, C, P], F32R)
        pick = sb("pick", [P, 2, P], F32R)
        bq_col = sb("bq_col", [P, C])
        bq1_col = sb("bq1_col", [P, C])
        nbq_col = sb("nbq_col", [P, C])
        cols = sb("cols", [P, 2])
        eps_col = sb("eps_col", [P, 3])
        stats = sb("stats", [P, TPG, 6])
        mv1 = sb("mv1", [P, TPG, 2])
        r1 = sb("r1", [P, TPG])
        nm1 = sb("nm1", [P, TPG])
        nr = sb("nr", [P, 3, TPG])
        r1_all = sb("r1_all", [P, NG * TPG])
        r1_g = sb("r1_g", [P, TPG])
        bn = sb("bn", [P, 3, 2, 6])
        mv = sb("mv", [P, 3, 2, 2])
        sd = sb("sd", [P, 4, 2])
        rs = sb("rs", [P, 4, 2])
        nm = sb("nm", [P, 3, 2])
        ssq = sb("ssq", [P, 2])

        k_hi, k_lo = kvw[:, 0, 0:2, :], kvw[:, 0, 2:4, :]
        x3_flat = x3_T[:].rearrange("p t s c n -> p t s (c n)")
        x1_hi = [kvw[:, 1, 0, :], kvw[:, 1, 1, :], x3_flat[:, 0, 0, :], x3_flat[:, 1, 0, :]]
        x1_lo = [kvw[:, 1, 2, :], kvw[:, 1, 3, :], x3_flat[:, 0, 1, :], x3_flat[:, 1, 1, :]]
        k1, e_k, k_f, e_q = (work[:, 2 * j:2 * j + 2, :] for j in range(4))
        h, x3 = (work[:, 2 * j:2 * j + 2, :] for j in range(2))
        junk = work[:, 7, :]
        den_sb = work[0:NH, 6, :]
        z_row = work[:, 4, :].rearrange("p (t n) -> p t n", t=TPG)
        kx_T = work[:, 0:4, :]
        cosm, sinm, wr_sb, wi_sb = (q_T[:, j, :].rearrange("p (c n) -> p c n", c=C) for j in range(4))
        ncos = work[:, 0:4, :]
        p_T, r_T = xb, x2

        banks = [ctx.enter_context(nc.psum_tensor(f"bank{i}", [P, D], F32)) for i in range(8)]
        kx_ps = banks[0:4]
        hs_ps = banks[0:2]
        den_ps, zrow_ps = banks[2], banks[3]
        zb_ps = [banks[3], banks[2]]
        mm_ps = banks[4:6]
        t_ps = banks[6:8]

        def setup_sems(names):
            return [sem(n) for n in names.split()]

        def made_by(names):
            return [sem(n) for n in names.split()]

        w_in, w_in2, w_in3, split_hi, split_done, pre, cols_ok, setup_done = setup_sems(
            "w_in w_in2 w_in3 split_hi split_done pre cols_ok setup_done")
        m1_ps, m1_act, m1_dve, m2_ps, m2_c, m2_hi, m2_out = setup_sems("m1_ps m1_act m1_dve m2_ps m2_c m2_hi m2_out")
        xa_in, xb_in = sems("xa_in"), sems("xb_in")
        dve_ln1, ln1_bn = sem("dve_ln1"), sem("ln1_bn")

        by_sp = out_st = sems("out_st")
        by_pool = made_by("kacc_zero kacc_ok gam_ok gb_ok qlo_ok") + sems("x1lo_ok")
        kacc_zero, kacc_ok, gam_ok, gb_ok, qlo_ok = by_pool[:5]
        x1lo_ok = by_pool[5:]
        by_act = made_by("xthi rq_ok eq_ok rk_ok ek_ok khi_ok x1hi_ok kx_act kvwhi den_ok zhi_ok qhi_ok "
                         "sd_ok0 sd_ok1 sd_ok2 sd_ok3 n_ok u_ok x3_ok x3hi ysq_ok") + sems("x1f_ok")
        xthi, rq_ok, eq_ok, rk_ok, ek_ok, khi_ok, x1hi_ok, kx_act, kvwhi, den_ok, zhi_ok, qhi_ok = by_act[:12]
        sd_ok, (n_ok, u_ok, x3_ok, x3hi, ysq_ok), x1f_ok = by_act[12:16], by_act[16:21], by_act[21:]
        by_dve = made_by("ln1_ok xtlo q_ok k1_ok k_ok klo_ok ksum_ok kx_dve kv_ok kvwlo z_ok zlo_ok qp_ok r1g_ok h_ok "
                         "bn_ok0 bn_ok1 bn_ok2 mv_ok0 mv_ok1 mv_ok2 rs_ok0 rs_ok1 rs_ok2 rs_ok3 nm_ok0 nm_ok1 nm_ok2 "
                         "x3lo fin_ok") + sems("x2_ok")
        ln1_ok, xtlo, q_ok, k1_ok, k_ok, klo_ok, ksum_ok, kx_dve, kv_ok, kvwlo, z_ok, zlo_ok, qp_ok, r1g_ok, h_ok = by_dve[:15]
        bn_ok, mv_ok, rs_ok, nm_ok, (x3lo, fin_ok), x2_ok = (by_dve[15:18], by_dve[18:21], by_dve[21:25], by_dve[25:28],
                                                             by_dve[28:30], by_dve[30:])
        by_pe = made_by("q_ps kx_done ksum_ps kv_ps kvw_ps d_ps dt_ps zt_ps zb_done hs_done x3t_ps y_ps") + sems("x1t_ps") + sems("k_ps")
        q_ps, kx_done, ksum_ps, kv_ps, kvw_ps, d_ps, dt_ps, zt_ps, zb_done, hs_done, x3t_ps, y_ps = by_pe[:12]
        x1t_ps, k_ps = by_pe[12:16], by_pe[16:]

        def start(eng, made):
            for one in made:
                eng.sem_inc(one, 1)

        chunked = lambda a: a.rearrange("(c p) n -> p c n", p=P)
        block = ctx.enter_context(nc.Block())

        @block.sync
        def _(sp):
            start(sp, by_sp)
            def load_xa(i, c, first_row):
                wait(sp, x1f_ok[i], c - 1)
                sp.dma_start(xa[:, i, :], x[bass.ds(first_row + i * P, P), :]).then_inc(xa_in[i], 16)

            def load_xb(i, c, first_row):
                wait(sp, x2_ok[i], c - 1)
                sp.dma_start(xb[:, i, :], x[bass.ds(first_row + i * P, P), :]).then_inc(xb_in[i], 16)

            def store(i, c, first_row):
                wait(sp, fin_ok, ticks(i, c))
                sp.dma_start(out[bass.ds(first_row + i * P, P), :], x2[:, i, :]).then_inc(out_st[i], 16)

            for dst, src in ((wr_sb, chunked(wr)), (wi_sb, chunked(wi)), (cosm, chunked(dft[0])),
                             (sinm, chunked(dft[1])), (ncos, chunked(dft[2])), (cst[:], consts)):
                sp.dma_start(dst, src).then_inc(w_in, 16)
            for i in range(TPG):
                load_xa(i, 1, 0)
            for dst, src in ((gamma_bc[:], gamma), (beta_bc[:], beta), (bk1_bc[:], bk), (bv_bc[:], bv)):
                sp.dma_start(dst, src.partition_broadcast(P)).then_inc(w_in2, 16)
            sp.dma_start(bq_col[:], bq).then_inc(w_in2, 16)
            sp.dma_start(den_sb, spread_f).then_inc(w_in2, 16)
            sp.dma_start(w_vT[:], chunked(wv)).then_inc(w_in2, 16)
            sp.dma_start(w_dT[:], chunked(wd)).then_inc(w_in2, 16)
            sp.dma_start(x1f[:], chunked(wq)).then_inc(w_in3, 16)
            sp.wait_ge(split_done, 1)
            sp.dma_start(x1f[:], chunked(wk)).then_inc(w_in3, 16)
            sp.wait_ge(split_done, 2)
            sp.dma_start(x1f[:, 0, :], fbias.partition_broadcast(P)).then_inc(w_in3, 16)
            sp.dma_start(x1f[:, 1, :], bd.partition_broadcast(P)).then_inc(w_in3, 16)
            sp.wait_ge(setup_done, 1)

            def batch(b, last):
                row = b * (NG * GR)
                for i in range(TPG):
                    load_xb(i, b * NG + 1, row)
                for g in range(NG):
                    wrapped = last and g == NG - 1
                    for i in range(TPG):
                        load_xa(i, b * NG + (g + 2), 0 if wrapped else row + (g + 1) * GR)
                for k in range(NG * TPG + TPG):
                    g, i = divmod(k, TPG)
                    if k >= TPG:
                        store(i, b * NG + g, row + (g - 1) * GR)
                    if g + 1 < NG:
                        load_xb(i, b * NG + (g + 2), row + (g + 1) * GR)

            with sp.Fori(0, B - 1) as b:
                batch(b, False)
            batch(B - 1, True)
            for i in range(TPG):
                wait(sp, out_st[i], 16 * B * NG)

        @block.gpsimd
        def _(pool):
            start(pool, by_pool)
            pool.memset(eps_col[:, 0:1], EPS_LN).then_inc(pre, 1)
            pool.memset(eps_col[:, 1:2], EPS_INNER).then_inc(pre, 1)
            pool.memset(eps_col[:, 2:3], 1.0).then_inc(pre, 1)

            def x1lo(i, c):
                wait(pool, x1hi_ok, ticks(i, c))
                pool.tensor_tensor(x1_lo[i], x1f[:, i, :], x1_hi[i], ALU.subtract).then_inc(x1lo_ok[i], 1)

            def kacc(i, c, b):
                wait(pool, k_ok, ticks(i, c))
                wait(pool, kacc_zero, b + 1)
                if i:
                    wait(pool, kacc_ok, ticks(i - 1, c))
                else:
                    wait(pool, kacc_ok, c * 4 - 4)
                pool.tensor_tensor(k_acc[:], k_acc[:], k_f[:, i % 2, :], ALU.add).then_inc(kacc_ok, 1)

            def affine(i, c):
                wait(pool, n_ok, ticks(i, c))
                pool.tensor_tensor(h[:, i % 2, :], h[:, i % 2, :], gamma_bc[:], ALU.mult).then_inc(gam_ok, 1)
                wait(pool, gam_ok, ticks(i, c))
                pool.tensor_tensor(h[:, i % 2, :], h[:, i % 2, :], beta_bc[:], ALU.add).then_inc(gb_ok, 1)

            def q_low(i, c, g):
                wait(pool, qhi_ok, ticks(i, c))
                s = slice(i * P, (i + 1) * P)
                pool.tensor_tensor(act_T[:, 1, :, s], q_T[:, :, bass.ds(g * GR + i * P, P)], act_T[:, 0, :, s],
                                   ALU.subtract).then_inc(qlo_ok, 1)

            pool.wait_ge(pre, 3)
            pool.wait_ge(setup_done, 1)
            with pool.Fori(0, B) as b:
                wait(pool, kv_ps, b)
                pool.tensor_tensor(cols[:], eps_col[:, 0:2], eps_col[:, 0:2], ALU.add)
                pool.memset(k_acc[:], 0.0).then_inc(kacc_zero, 1)
                with pool.Fori(0, NG) as g:
                    c = pool.snap(b * NG + g + 1)
                    for i in range(TPG):
                        x1lo(i, c)
                    for i in range(TPG):
                        kacc(i, c, b)
                c0 = pool.snap(b * NG + 1)
                q_low(0, c0, 0)
                with pool.Fori(0, NG - 1) as g:
                    c = pool.snap(b * NG + g + 1)
                    for i in range(3):
                        q_low(i + 1, c, g)
                        affine(i, c)
                    q_low(0, c + 1, g + 1)
                    affine(3, c)
                c3 = pool.snap(b * NG + NG)
                for i in range(3):
                    q_low(i + 1, c3, NG - 1)
                    affine(i, c3)
                affine(3, c3)

        @block.scalar
        def _(act):
            start(act, by_act)

            def copy(dst, src):
                return act.activation(dst, src, ACT.Copy)

            def make_x1f(i, c):
                wait(act, ln1_ok, c)
                wait(act, x1t_ps[i], c - 1)
                wait(act, x1lo_ok[i], c - 1)
                act.activation(x1f[:, i, :], xa[:, i, :], ACT.Identity, bias=nm1[:, i:i + 1], scale=r1[:, i:i + 1]).then_inc(x1f_ok[i], 1)

            def xt_hi(i, c):
                wait(act, x1t_ps[i], c)
                wait(act, k_ps[i], c - 1)
                copy(act_T[:, 0, :, i * P:(i + 1) * P], t_ps[i % 2][:].rearrange("p (c n) -> p c n", c=C)).then_inc(xthi, 1)

            def exp_q(u, c):
                wait(act, q_ps, ticks(u, c))
                wait(act, q_ok, two_back(u, c))
                act.activation(e_q[:, u % 2, :], mm_ps[u % 2][:], ACT.Relu, bias=nbq_col[:, u:u + 1], scale=-1.0).then_inc(rq_ok, 1)
                wait(act, rq_ok, ticks(u, c))
                act.activation(e_q[:, u % 2, :], e_q[:, u % 2, :], ACT.Exp, scale=-1.0).then_inc(eq_ok, 1)

            def split_x1(i, c, b):
                wait(act, kx_done, c * 4 - 4)
                wait(act, y_ps, b * (NG * TPG))
                wait(act, x1f_ok[i], c)
                copy(x1_hi[i], x1f[:, i, :]).then_inc(x1hi_ok, 1)

            def exp_k(i, c):
                wait(act, k1_ok, ticks(i, c))
                wait(act, k_ok, two_back(i, c))
                act.activation(e_k[:, i % 2, :], k1[:, i % 2, :], ACT.Relu, bias=eps_col[:, 2:3], scale=-1.0).then_inc(rk_ok, 1)
                wait(act, rk_ok, ticks(i, c))
                act.activation(e_k[:, i % 2, :], e_k[:, i % 2, :], ACT.Exp, scale=-1.0).then_inc(ek_ok, 1)

            def split_k(i, c):
                wait(act, k_ok, ticks(i, c))
                wait(act, kx_done, two_back(i, c))
                copy(k_hi[:, i % 2, :], k_f[:, i % 2, :]).then_inc(khi_ok, 1)

            def copy_den(c):
                wait(act, d_ps, c)
                wait(act, dt_ps, c - 1)
                copy(den_sb, den_ps[0:NH, :]).then_inc(den_ok, 1)

            def z_hi(c):
                wait(act, zt_ps, c)
                wait(act, zb_done, c * 4 - 4)
                copy(z_hl[:, 0, :], den_ps[0:NH, :]).then_inc(zhi_ok, 1)

            def q_hi(i, c, g, before):
                wait(act, qp_ok, c * 4)
                wait(act, hs_done, before)
                copy(act_T[:, 0, :, i * P:(i + 1) * P], q_T[:, :, bass.ds(g * GR + i * P, P)]).then_inc(qhi_ok, 1)

            def root(j, i, c, eps):
                wait(act, mv_ok[j], ticks(i, c))
                act.activation(sd[:, j, i % 2:i % 2 + 1], mv[:, j, i % 2, 1:2], ACT.Sqrt, bias=eps_col[:, eps:eps + 1]).then_inc(sd_ok[j], 1)

            def normalise(j, i, c, dst, src, done):
                wait(act, nm_ok[j], ticks(i, c))
                act.activation(dst, src, ACT.Identity, bias=nm[:, j, i % 2:i % 2 + 1], scale=rs[:, j, i % 2:i % 2 + 1]).then_inc(done, 1)

            def make_x3(i, c):
                wait(act, x3t_ps, two_back(i, c))
                normalise(2, i, c, x3[:, i % 2, :], x2[:, i, :], x3_ok)

            def x3_hi(i, c):
                wait(act, x3t_ps, ticks(i, c))
                wait(act, y_ps, two_back(i, c))
                copy(x3_T[:, i % 2, 0, :, :], t_ps[i % 2][:].rearrange("p (c n) -> p c n", c=C)).then_inc(x3hi, 1)

            def y_root(i, c):
                wait(act, y_ps, ticks(i, c))
                act.activation(junk, mm_ps[i % 2][:], ACT.Square, accum_out=ssq[:, i % 2:i % 2 + 1]).then_inc(ysq_ok, 1)
                wait(act, ysq_ok, ticks(i, c))
                act.activation(sd[:, 3, i % 2:i % 2 + 1], ssq[:, i % 2:i % 2 + 1], ACT.Sqrt, bias=eps_col[:, 0:1], scale=1.0 / D).then_inc(sd_ok[3], 1)

            act.wait_ge(pre, 3)
            for n, w in enumerate((w_qT, w_kT)):
                act.wait_ge(w_in3, 16 * (n + 1))
                copy(w[:, 0], x1f[:]).then_inc(split_hi, 1)
            for n in range(C):
                act.wait_ge(m1_ps, 2 * n + 1)
                copy(p_T[:, n, :], banks[0 + 2 * (n % 2)][:]).then_inc(m1_act, 1)
            for n in range(C):
                act.wait_ge(m2_c, n + 1)
                copy(w_m[:, 0, n, :], work[:, 4 + n, :]).then_inc(m2_hi, 1)
            act.wait_ge(setup_done, 1)
            for i in range(TPG):
                make_x1f(i, 1)
            for i in range(TPG):
                xt_hi(i, 1)

            def phase1(c, b, more):
                exp_q(0, c)
                exp_q(1, c)
                split_x1(0, c, b)
                split_x1(1, c, b)
                exp_q(2, c)
                split_x1(2, c, b)
                split_x1(3, c, b)
                exp_q(3, c)
                make_x1f(0, c + 1)
                make_x1f(1, c + 1)
                for i in range(TPG):
                    exp_k(i, c)
                    if i < 2:
                        make_x1f(i + 2, c + 1)
                    if more:
                        xt_hi(i, c + 1)
                    split_k(i, c)

            def slot(i, c, here, before, t, f, coming=None, den=None, z=None):
                if t is not None:
                    x3_hi(*t)
                if coming is not None:
                    q_hi(*coming)
                if den is not None:
                    copy_den(den)
                if f is not None:
                    y_root(*f)
                if before:
                    j, cj = (i - 1, c) if i else (TPG - 1, c - 1)
                    root(1, j, cj, 0)
                    normalise(1, j, cj, h[:, j % 2, :], h[:, j % 2, :], u_ok)
                if z is not None:
                    z_hi(z)
                if here:
                    root(0, i, c, 1)
                    normalise(0, i, c, h[:, i % 2, :], h[:, i % 2, :], n_ok)
                if before:
                    root(2, j, cj, 0)
                    make_x3(j, cj)

            def phase2(c, g, prev, more):
                p = c - 1
                done = c * 4 - 4
                slot(0, c, True, prev, (1, p) if prev else None, (0, p) if prev else None, (1, c, g, done), c + 1 if more else None)
                slot(1, c, True, True, (2, p) if prev else None, (1, p) if prev else None, (2, c, g, done), None, c + 1 if more else None)
                slot(2, c, True, True, (3, p) if prev else None, (2, p) if prev else None, (3, c, g, done))
                slot(3, c, True, True, (0, c), (3, p) if prev else None, (0, c + 1, g + 1, c * 4 - 3) if more else None)

            with act.Fori(0, B) as b:
                with act.Fori(0, NG - 1) as g:
                    phase1(act.snap(b * NG + g + 1), b, True)
                c3 = act.snap(b * NG + NG)
                phase1(c3, b, False)
                wait(act, kx_done, c3 * 4)
                for j in (0, 2):
                    copy(kx_T[:, j, :], kx_ps[j][:]).then_inc(kx_act, 1)
                c0 = act.snap(b * NG + 1)
                copy_den(c0)
                z_hi(c0)
                for u in range(C):
                    wait(act, kvw_ps, b * C + (u + 1))
                    copy(kvw[:, 0, u, :], banks[u][:]).then_inc(kvwhi, 1)
                q_hi(0, c0, 0, c0 * 4 - 4)
                phase2(c0, 0, False, True)
                with act.Fori(1, NG - 1) as g:
                    phase2(act.snap(b * NG + g + 1), g, True, True)
                c3 = act.snap(b * NG + NG)
                phase2(c3, NG - 1, True, False)
                slot(0, c3 + 1, False, True, (1, c3), (0, c3))
                slot(1, c3 + 1, False, False, (2, c3), (1, c3))
                xt_hi(0, c3 + 1)
                slot(2, c3 + 1, False, False, (3, c3), (2, c3))
                for i in range(1, TPG):
                    xt_hi(i, c3 + 1)
                y_root(3, c3)

        @block.vector
        def _(dve):
            start(dve, by_dve)
            dve.wait_ge(w_in2, 16 * 8)
            dve.tensor_scalar(bk1_bc[:], bk1_bc[:], 1.0, None, ALU.add)
            dve.tensor_scalar(bq1_col[:], bq_col[:], 1.0, None, ALU.add)
            dve.tensor_scalar(nbq_col[:], bq_col[:], -1.0, None, ALU.mult)
            dve.wait_ge(w_in, 16 * 6)
            dve.tensor_tensor(cols[:, 0:1], ident[:, 0:1], ident[:, 1:2], ALU.add)
            dve.tensor_tensor(cols[:, 1:2], ident[:, 2:3], ident[:, 3:4], ALU.add).then_inc(cols_ok, 1)
            dve.wait_ge(cols_ok, 1)
            for n in range(2):
                dve.tensor_scalar(pick[:, n, :], ones, cols[:, n:n + 1], None, ALU.mult)
            dve.tensor_copy(spread[:], den_sb.rearrange("h (u n) -> h u n", u=C))
            for n, w in enumerate((w_qT, w_kT)):
                dve.wait_ge(split_hi, n + 1)
                dve.tensor_tensor(w[:, 1], x1f[:], w[:, 0], ALU.subtract).then_inc(split_done, 1)
            for n in range(C):
                dve.wait_ge(m1_ps, 2 * n + 2)
                dve.tensor_copy(r_T[:, n, :], banks[1 + 2 * (n % 2)][:]).then_inc(m1_dve, 1)
            setup_steps = [0]

            def link(ins):
                setup_steps[0] += 1
                ins.then_inc(m2_out, 1)
                dve.wait_ge(m2_out, setup_steps[0])

            def centre(dst, src, scale):
                link(dve.bn_stats(bn[:, 0, 0, :], src))
                link(dve.bn_aggr(mv[:, 0, 0, :], bn[:, 0, 0, :]))
                return dve.tensor_scalar(dst, src, mv[:, 0, 0, 0:1], scale, ALU.subtract, ALU.mult)

            for n in range(C):
                dve.wait_ge(m2_ps, n + 1)
                centre(work[:, 4 + n, :], banks[4 + n % 2][:], 1.0 / D).then_inc(m2_c, 1)
                dve.wait_ge(m2_hi, n + 1)
                link(dve.tensor_tensor(w_m[:, 1, n, :], work[:, 4 + n, :], w_m[:, 0, n, :], ALU.subtract))
            fb, bd_b, acc, hi_f = x1f[:, 0, :], x1f[:, 1, :], x1f[:, 2, :], x1f[:, 3, :]
            dve.wait_ge(w_in3, 16 * 4)
            link(centre(fb, fb, 1.0))
            link(dve.memset(acc, 0.0))
            for n, bias in enumerate((fb, bd_b)):
                link(dve.tensor_copy(bias_rows[:], bias))
                link(dve.tensor_copy(hi_f, bias_rows[:]))
                link(dve.tensor_tensor(bias, bias, hi_f, ALU.subtract))
                for part, row in ((hi_f, 2 * n), (bias, 2 * n + 1)):
                    link(dve.scalar_tensor_tensor(out=acc, in0=part, scalar=ident[:, row:row + 1], in1=acc, op0=ALU.mult, op1=ALU.add))
            dve.tensor_copy(bias_rows[:], acc).then_inc(setup_done, 1)

            def ln1_stats(i, c):
                dve.wait_ge(xa_in[i], c * 16)
                dve.bn_stats(stats[:, i, :], xa[:, i, :]).then_inc(ln1_bn, 1)

            LN1_STEPS = 2 + 3 * NEWTON + 2

            def ln1_finish(c, g=None):
                n = [0]

                def step(ins):
                    n[0] += 1
                    ins.then_inc(dve_ln1, 1)
                    dve.wait_ge(dve_ln1, (c - 1) * LN1_STEPS + n[0])

                dve.wait_ge(ln1_bn, c * 4)
                if g is not None:
                    dve.tensor_copy(r1_all[:, bass.ds(g * TPG, TPG)], r1[:])
                for i in range(TPG):
                    ins = dve.bn_aggr(mv1[:, i, :], stats[:, i, :])
                step(ins)
                v, y, a = nr[:, 0, :], nr[:, 1, :], nr[:, 2, :]
                step(dve.tensor_scalar(v, mv1[:, :, 1], EPS_LN, None, ALU.add))
                step(dve.tensor_scalar(a.bitcast(U32), v.bitcast(U32), 1, None, ALU.logical_shift_right))
                wait(dve, x1f_ok[3], c - 1)
                step(dve.tensor_scalar(y.bitcast(I32), a.bitcast(I32), -1, RSQRT_MAGIC, ALU.mult, ALU.add))
                for s in range(NEWTON):
                    step(dve.scalar_tensor_tensor(out=a, in0=y, scalar=-0.5, in1=v, op0=ALU.mult, op1=ALU.mult))
                    step(dve.tensor_tensor(a, a, y, ALU.mult))
                    last = s == NEWTON - 1
                    step(dve.scalar_tensor_tensor(out=r1[:] if last else y, in0=a, scalar=1.5, in1=y, op0=ALU.add, op1=ALU.mult))
                assert n[0] == LN1_STEPS
                dve.scalar_tensor_tensor(out=nm1[:], in0=mv1[:, :, 0], scalar=-1.0, in1=r1[:], op0=ALU.mult,
                                         op1=ALU.mult).then_inc(ln1_ok, 1)

            def xt_lo(i, c):
                wait(dve, xthi, ticks(i, c))
                s = slice(i * P, (i + 1) * P)
                dve.tensor_tensor(act_T[:, 1, :, s], t_ps[i % 2][:].rearrange("p (c n) -> p c n", c=C),
                                  act_T[:, 0, :, s], ALU.subtract).then_inc(xtlo, 1)

            def q_feature(u, c, g):
                wait(dve, eq_ok, ticks(u, c))
                dve.scalar_tensor_tensor(out=q_T[:, u, bass.ds(g * GR, GR)], in0=mm_ps[u % 2][:], scalar=bq1_col[:, u:u + 1],
                                         in1=e_q[:, u % 2, :], op0=ALU.add, op1=ALU.max).then_inc(q_ok, 1)

            def k_bias(i, c):
                wait(dve, k_ps[i], c)
                wait(dve, ek_ok, two_back(i, c))
                dve.tensor_tensor(k1[:, i % 2, :], mm_ps[i % 2][:], bk1_bc[:], ALU.add).then_inc(k1_ok, 1)

            def k_feature(i, c):
                wait(dve, ek_ok, ticks(i, c))
                wait(dve, kacc_ok, two_back(i, c))
                wait(dve, khi_ok, two_back(i, c))
                dve.tensor_tensor(k_f[:, i % 2, :], e_k[:, i % 2, :], k1[:, i % 2, :], ALU.max).then_inc(k_ok, 1)

            def k_low(i, c):
                wait(dve, khi_ok, ticks(i, c))
                dve.tensor_tensor(k_lo[:, i % 2, :], k_f[:, i % 2, :], k_hi[:, i % 2, :], ALU.subtract).then_inc(klo_ok, 1)

            def phase1(c, g, more):
                for i in range(TPG):
                    ln1_stats(i, c + 1)
                q_feature(0, c, g)
                ln1_finish(c + 1, g)
                for u in range(1, C):
                    q_feature(u, c, g)
                k_bias(0, c)
                for i in range(TPG):
                    k_feature(i, c)
                    if more:
                        xt_lo(i, c + 1)
                    if i + 1 < TPG:
                        k_bias(i + 1, c)
                    k_low(i, c)

            def invert(c):
                wait(dve, dt_ps, c)
                wait(dve, zt_ps, c - 1)
                dve.reciprocal(z_row[:, :, 0:NH], zrow_ps[:, 0:TPG * NH].rearrange("p (t h) -> p t h", h=NH)).then_inc(z_ok, 1)

            def z_low(c):
                wait(dve, zhi_ok, c)
                dve.tensor_tensor(z_hl[:, 1, :], den_ps[0:NH, :], z_hl[:, 0, :], ALU.subtract).then_inc(zlo_ok, 1)

            def q_scaled(u, c, g):
                wait(dve, zb_done, ticks(u, c))
                rows = bass.ds(g * GR, GR)
                dve.tensor_tensor(q_T[:, u, rows], zb_ps[u % 2][:], q_T[:, u, rows], ALU.mult).then_inc(qp_ok, 1)

            def residual(i, c):
                wait(dve, hs_done, ticks(i, c))
                dve.wait_ge(xb_in[i], c * 16)
                wait(dve, r1g_ok, c)
                dve.scalar_tensor_tensor(out=h[:, i % 2, :], in0=xb[:, i, :], scalar=r1_g[:, i:i + 1], in1=hs_ps[i % 2][:],
                                         op0=ALU.mult, op1=ALU.add).then_inc(h_ok, 1)

            def stats_of(j, i, src):
                dve.bn_stats(bn[:, j, i % 2, :], src).then_inc(bn_ok[j], 1)

            def moments(j, i, c):
                wait_apart(dve, bn_ok[j], ticks(i, c), pre, 3)
                dve.bn_aggr(mv[:, j, i % 2, :], bn[:, j, i % 2, :]).then_inc(mv_ok[j], 1)

            def scales(j, i, c):
                wait(dve, sd_ok[j], ticks(i, c))
                dve.reciprocal(rs[:, j, i % 2:i % 2 + 1], sd[:, j, i % 2:i % 2 + 1]).then_inc(rs_ok[j], 1)
                wait(dve, rs_ok[j], ticks(i, c))
                dve.scalar_tensor_tensor(out=nm[:, j, i % 2:i % 2 + 1], in0=mv[:, j, i % 2, 0:1], scalar=-1.0,
                                         in1=rs[:, j, i % 2:i % 2 + 1], op0=ALU.mult, op1=ALU.mult).then_inc(nm_ok[j], 1)

            def add_x(i, c):
                wait(dve, u_ok, ticks(i, c))
                wait(dve, out_st[i], c * 16 - 16)
                dve.tensor_tensor(x2[:, i, :], xb[:, i, :], h[:, i % 2, :], ALU.add).then_inc(x2_ok[i], 1)
                wait(dve, x2_ok[i], c)

            def x3_low(i, c):
                wait(dve, x3hi, ticks(i, c))
                dve.tensor_tensor(x3_T[:, i % 2, 1, :, :], t_ps[i % 2][:].rearrange("p (c n) -> p c n", c=C),
                                  x3_T[:, i % 2, 0, :, :], ALU.subtract).then_inc(x3lo, 1)

            def finish(i, c):
                wait(dve, sd_ok[3], ticks(i, c))
                dve.reciprocal(rs[:, 3, i % 2:i % 2 + 1], sd[:, 3, i % 2:i % 2 + 1]).then_inc(rs_ok[3], 1)
                wait(dve, rs_ok[3], ticks(i, c))
                dve.scalar_tensor_tensor(out=x2[:, i, :], in0=mm_ps[i % 2][:], scalar=rs[:, 3, i % 2:i % 2 + 1],
                                         in1=x2[:, i, :], op0=ALU.mult, op1=ALU.add).then_inc(fin_ok, 1)

            def slot(i, c, here, before, t, f, z=None):
                if t is not None:
                    x3_low(*t)
                if before:
                    j, cj = (i - 1, c) if i else (TPG - 1, c - 1)
                    wait(dve, gb_ok, ticks(j, cj))
                    stats_of(1, j, h[:, j % 2, :])
                if f is not None:
                    finish(*f)
                if before:
                    moments(1, j, cj)
                if here:
                    residual(i, c)
                if before:
                    scales(1, j, cj)
                if here:
                    wait(dve, h_ok, ticks(i, c))
                    stats_of(0, i, h[:, i % 2, :])
                    moments(0, i, c)
                if before:
                    add_x(j, cj)
                if here:
                    scales(0, i, c)
                if before:
                    stats_of(2, j, x2[:, j, :])
                if z is not None:
                    z_low(z)
                if before:
                    moments(2, j, cj)
                    scales(2, j, cj)

            def phase2(c, g, prev, more):
                p = c - 1
                dve.tensor_copy(r1_g[:], r1_all[:, bass.ds(g * TPG, TPG)]).then_inc(r1g_ok, 1)
                slot(0, c, True, prev, (1, p) if prev else None, (0, p) if prev else None)
                if more:
                    invert(c + 1)
                slot(1, c, True, True, (2, p) if prev else None, (1, p) if prev else None, c + 1 if more else None)
                if more:
                    q_scaled(0, c + 1, g + 1)
                    q_scaled(1, c + 1, g + 1)
                slot(2, c, True, True, (3, p) if prev else None, (2, p) if prev else None)
                if more:
                    q_scaled(2, c + 1, g + 1)
                    q_scaled(3, c + 1, g + 1)
                slot(3, c, True, True, (0, c), (3, p) if prev else None)

            for i in range(TPG):
                ln1_stats(i, 1)
            ln1_finish(1)
            for i in range(TPG):
                xt_lo(i, 1)

            with dve.Fori(0, B) as b:
                with dve.Fori(0, NG - 1) as g:
                    phase1(dve.snap(b * NG + g + 1), g, True)
                c3 = dve.snap(b * NG + NG)
                phase1(c3, NG - 1, False)
                wait(dve, kx_done, c3 * 4)
                for j in (1, 3):
                    dve.tensor_copy(kx_T[:, j, :], kx_ps[j][:]).then_inc(kx_dve, 1)
                mask4 = head_mask.unsqueeze(1).broadcast_to([P, C, P])
                wait(dve, ksum_ps, b + 1)
                dve.scalar_tensor_tensor(out=ksum_h[:], in0=t_ps[1][:, 0:C * NH].rearrange("p (u h) -> p u h", h=NH), scalar=EPS_ATTN,
                                         in1=own_head, op0=ALU.add, op1=ALU.mult).then_inc(ksum_ok, 1)
                c0 = dve.snap(b * NG + 1)
                invert(c0)
                z_low(c0)
                for u in range(C):
                    q_scaled(u, c0, 0)
                wait(dve, kv_ps, b + 1)
                dve.tensor_tensor(kv_T[:], t_ps[0][:].rearrange("p (c n) -> p c n", c=C), mask4, ALU.mult).then_inc(kv_ok, 1)
                for u in range(C):
                    wait(dve, kvwhi, b * C + (u + 1))
                    dve.tensor_tensor(kvw[:, 1, u, :], banks[u][:], kvw[:, 0, u, :], ALU.subtract).then_inc(kvwlo, 1)
                phase2(c0, 0, False, True)
                with dve.Fori(1, NG - 1) as g:
                    phase2(dve.snap(b * NG + g + 1), g, True, True)
                c3 = dve.snap(b * NG + NG)
                phase2(c3, NG - 1, True, False)
                slot(0, c3 + 1, False, True, (1, c3), (0, c3))
                slot(1, c3 + 1, False, False, (2, c3), (1, c3))
                xt_lo(0, c3 + 1)
                slot(2, c3 + 1, False, False, (3, c3), (2, c3))
                for i in range(1, TPG):
                    xt_lo(i, c3 + 1)
                finish(3, c3)

        @block.tensor
        def _(pe):
            start(pe, by_pe)

            def split_product(dst, left_hi, left_lo, right_hi, right_lo, start, stop, **kw):
                pe.matmul(dst, left_hi, right_hi, start=start, stop=False, **kw)
                pe.matmul(dst, left_hi, right_lo, start=False, stop=False, **kw)
                return pe.matmul(dst, left_lo, right_hi, start=False, stop=stop, **kw)

            pe.wait_ge(w_in, 16 * 6)
            for n in range(C):
                o = slice(n * P, (n + 1) * P)
                if n >= 2:
                    pe.wait_ge(m1_act, n - 1)
                    pe.wait_ge(m1_dve, n - 1)
                for bank, right_r, right_i in ((banks[2 * (n % 2)], cosm, sinm), (banks[2 * (n % 2) + 1], sinm, ncos)):
                    for j in range(C):
                        pe.matmul(bank[:], wr_sb[:, j, o], right_r[:, j, :], start=(j == 0), stop=False)
                        mm = pe.matmul(bank[:], wi_sb[:, j, o], right_i[:, j, :], start=False, stop=(j == C - 1))
                    mm.then_inc(m1_ps, 1)
            pe.wait_ge(m1_act, C)
            pe.wait_ge(m1_dve, C)
            for n in range(C):
                o = slice(n * P, (n + 1) * P)
                if n >= 2:
                    pe.wait_ge(m2_c, n - 1)
                for j in range(C):
                    pe.matmul(banks[4 + n % 2][:], p_T[:, j, o], cosm[:, j, :], start=(j == 0), stop=False)
                    mm = pe.matmul(banks[4 + n % 2][:], r_T[:, j, o], sinm[:, j, :], start=False, stop=(j == C - 1))
                mm.then_inc(m2_ps, 1)

            def transpose_x1(i, c):
                wait(pe, x1f_ok[i], c)
                wait(pe, xtlo, two_back(i, c))
                for j in range(C):
                    mm = pe.transpose(t_ps[i % 2][:, j * P:(j + 1) * P], x1f[:, i, j * P:(j + 1) * P], ident)
                mm.then_inc(x1t_ps[i], 1)

            def project_q(u, c, b):
                wait(pe, xtlo, c * 4)
                if u < 2:
                    wait(pe, k1_ok, c * 4 - 4)
                    wait(pe, fin_ok, b * (NG * TPG))
                else:
                    wait(pe, q_ok, ticks(u - 2, c))
                for j in range(C):
                    o = slice(u * P, (u + 1) * P)
                    mm = split_product(mm_ps[u % 2][:], w_qT[:, 0, j, o], w_qT[:, 1, j, o], act_T[:, 0, j, :], act_T[:, 1, j, :],
                                       j == 0, j == C - 1)
                mm.then_inc(q_ps, 1)

            def project_k(i, c):
                if i < 2:
                    wait(pe, q_ok, ticks(i + 2, c))
                else:
                    wait(pe, k1_ok, ticks(i - 2, c))
                for j in range(C):
                    s = slice(i * P, (i + 1) * P)
                    mm = split_product(mm_ps[i % 2][:], act_T[:, 0, j, s], act_T[:, 1, j, s], w_kT[:, 0, j, :], w_kT[:, 1, j, :],
                                       j == 0, j == C - 1)
                mm.then_inc(k_ps[i], 1)

            def outer_kx(i, c, first):
                wait(pe, x1lo_ok[i], c)
                wait(pe, klo_ok, ticks(i, c))
                for j in range(C):
                    o = slice(j * P, (j + 1) * P)
                    mm = split_product(kx_ps[j][:], x1_hi[i][:, o], x1_lo[i][:, o], k_hi[:, i % 2, :], k_lo[:, i % 2, :],
                                       first, False, skip_group_check=True)
                mm.then_inc(kx_done, 1)

            def phase1(c, b, first, more):
                project_q(0, c, b)
                if not first:
                    outer_kx(2, c - 1, False)
                project_q(1, c, b)
                if not first:
                    outer_kx(3, c - 1, False)
                project_q(2, c, b)
                project_q(3, c, b)
                project_k(0, c)
                if more:
                    transpose_x1(0, c + 1)
                project_k(1, c)
                if more:
                    transpose_x1(1, c + 1)
                project_k(2, c)
                if more:
                    transpose_x1(2, c + 1)
                outer_kx(0, c, first)
                project_k(3, c)
                if more:
                    transpose_x1(3, c + 1)
                outer_kx(1, c, False)

            def denominators(c, g):
                wait(pe, qp_ok, c * 4 - 4)
                for u in range(C):
                    mm = pe.matmul(den_ps[0:NH, :], ksum_h[:, u, :], q_T[:, u, bass.ds(g * GR, GR)], start=(u == 0), stop=(u == C - 1))
                mm.then_inc(d_ps, 1)

            def turn_denominators(c):
                wait(pe, den_ok, c)
                pe.matmul(zrow_ps[:, 0:NH], ident, ones[:, 0:NH], start=True, stop=True)
                for t in range(TPG):
                    mm = pe.transpose(zrow_ps[:, t * NH:(t + 1) * NH], den_sb[:, t * P:(t + 1) * P], ident[0:NH, 0:NH])
                mm.then_inc(dt_ps, 1)

            def turn_back(c):
                wait(pe, z_ok, c)
                for t in range(TPG):
                    mm = pe.transpose(den_ps[:, t * P:(t + 1) * P], z_row[:, t, :], ident)
                mm.then_inc(zt_ps, 1)

            def spread_z(u, c):
                wait(pe, zlo_ok, c)
                if u >= 2:
                    wait(pe, qp_ok, ticks(u - 2, c))
                pe.matmul(zb_ps[u % 2][:], spread[:, u, :], z_hl[:, 0, :], start=True, stop=False)
                pe.matmul(zb_ps[u % 2][:], spread[:, u, :], z_hl[:, 1, :], start=False, stop=True).then_inc(zb_done, 1)

            def attention(i, c):
                wait(pe, qlo_ok, ticks(i, c))
                wait(pe, h_ok, two_back(i, c))
                pe.matmul(hs_ps[i % 2][:], pick[:, 1, :], bias_rows[:], start=True, stop=False)
                for u in range(C):
                    s = slice(i * P, (i + 1) * P)
                    mm = split_product(hs_ps[i % 2][:], act_T[:, 0, u, s], act_T[:, 1, u, s], kvw[:, 0, u, :], kvw[:, 1, u, :],
                                       False, u == C - 1)
                mm.then_inc(hs_done, 1)

            def transpose_x3(i, c):
                wait(pe, x3_ok, ticks(i, c))
                wait(pe, x3lo, two_back(i, c))
                for j in range(C):
                    mm = pe.transpose(t_ps[i % 2][:, j * P:(j + 1) * P], x3[:, i % 2, j * P:(j + 1) * P], ident)
                mm.then_inc(x3t_ps, 1)

            def ffn(i, c):
                wait(pe, x3lo, ticks(i, c))
                wait(pe, fin_ok, two_back(i, c))
                pe.matmul(mm_ps[i % 2][:], pick[:, 0, :], bias_rows[:], start=True, stop=False)
                for j in range(C):
                    mm = split_product(mm_ps[i % 2][:], x3_T[:, i % 2, 0, j, :], x3_T[:, i % 2, 1, j, :], w_m[:, 0, j, :], w_m[:, 1, j, :],
                                       False, j == C - 1)
                mm.then_inc(y_ps, 1)

            def phase2(c, g, prev, more):
                if more:
                    denominators(c + 1, g + 1)
                if prev:
                    transpose_x3(1, c - 1)
                attention(0, c)
                if more:
                    turn_denominators(c + 1)
                if prev:
                    ffn(1, c - 1)
                    transpose_x3(2, c - 1)
                attention(1, c)
                if more:
                    turn_back(c + 1)
                if prev:
                    ffn(2, c - 1)
                    transpose_x3(3, c - 1)
                if more:
                    spread_z(0, c + 1)
                    spread_z(1, c + 1)
                attention(2, c)
                if more:
                    spread_z(2, c + 1)
                    spread_z(3, c + 1)
                if prev:
                    ffn(3, c - 1)
                transpose_x3(0, c)
                attention(3, c)
                ffn(0, c)

            pe.wait_ge(setup_done, 1)
            for i in range(TPG):
                transpose_x1(i, 1)

            with pe.Fori(0, B) as b:
                wait(pe, h_ok, b * (NG * TPG))
                wait(pe, qp_ok, b * (NG * TPG))
                phase1(pe.snap(b * NG + 1), b, True, True)
                with pe.Fori(1, NG - 1) as g:
                    phase1(pe.snap(b * NG + g + 1), b, False, True)
                c3 = pe.snap(b * NG + NG)
                phase1(c3, b, False, False)

                outer_kx(2, c3, False)
                outer_kx(3, c3, False)

                wait(pe, kacc_ok, c3 * 4)
                wait(pe, xtlo, c3 * 4)
                for u in range(C):
                    mm = pe.matmul(t_ps[1][:, u * NH:(u + 1) * NH], k_acc[:, u * P:(u + 1) * P], ones[:, 0:NH], start=True, stop=True)
                mm.then_inc(ksum_ps, 1)
                wait(pe, kx_act, b * 2 + 2)
                wait(pe, kx_dve, b * 2 + 2)
                wait(pe, ksum_ok, b + 1)
                c0 = pe.snap(b * NG + 1)
                denominators(c0, 0)
                turn_denominators(c0)
                for u in range(C):
                    if u == 1:
                        turn_back(c0)
                    if u == 3:
                        spread_z(0, c0)
                        spread_z(1, c0)
                    o = slice(u * P, (u + 1) * P)
                    for j in range(C):
                        pe.matmul(t_ps[0][:, o], w_vT[:, j, o], kx_T[:, j, o], start=(j == 0), stop=False)
                    mm = pe.matmul(t_ps[0][:, o], bv_bc[:, o], k_acc[:, o], start=False, stop=True)
                mm.then_inc(kv_ps, 1)
                spread_z(2, c0)
                spread_z(3, c0)
                wait(pe, kv_ok, b + 1)
                wait(pe, qp_ok, c0 * 4)
                for u in range(C):
                    pe.matmul(banks[u][:], kv_T[:, u, :], w_dT[:, u, :], start=True, stop=True).then_inc(kvw_ps, 1)
                wait(pe, kvwlo, b * C + C)
                phase2(c0, 0, False, True)
                with pe.Fori(1, NG - 1) as g:
                    phase2(pe.snap(b * NG + g + 1), g, True, True)
                c3 = pe.snap(b * NG + NG)
                phase2(c3, NG - 1, True, False)
                transpose_x3(1, c3)
                ffn(1, c3)
                transpose_x3(2, c3)
                wait(pe, x3lo, c3 * 4 - 1)
                transpose_x1(0, c3 + 1)
                ffn(2, c3)
                transpose_x3(3, c3)
                wait(pe, x3lo, c3 * 4)
                transpose_x1(1, c3 + 1)
                ffn(3, c3)
                transpose_x1(2, c3 + 1)
                transpose_x1(3, c3 + 1)


def constants():
    import numpy as np
    d = 512
    jk = np.outer(np.arange(d), np.arange(d)) % d
    cos, sin = np.cos(2 * np.pi * jk / d), np.sin(2 * np.pi * jk / d)
    dft = np.stack([cos, sin, -cos]).astype(np.float32)
    own = (np.arange(d) // 32)[:, None] == np.arange(16)[None, :]
    head = np.arange(P) // 32
    consts = np.concatenate([np.eye(P), head[:, None] == head[None, :], np.ones((P, P)),
                             own.reshape(4, P, 16).transpose(1, 0, 2).reshape(P, 64)], axis=1).astype(np.float32)
    return dft, np.ascontiguousarray(consts), np.ascontiguousarray(own.T.astype(np.float32))


def kernel(**inputs):
    import numpy as np
    import concourse.bacc as bacc
    from concourse.bass_utils import run_bass_kernel_spmd

    a = {k[3:]: np.asarray(v) for k, v in inputs.items()}
    x = np.ascontiguousarray(a["attn_input_tensor"]).reshape(-1, 512)
    dft, consts, spread_f = constants()
    arrays = {"x": x}
    for n, key in (("wq", "attn_Wq"), ("wk", "attn_Wk"), ("wv", "attn_Wv"), ("wd", "attn_Wd")):
        arrays[n] = np.ascontiguousarray(a[key].T)
    arrays["bq"] = np.ascontiguousarray(a["attn_bq"].reshape(4, P).T)
    for n, key in (("bk", "attn_bk"), ("bv", "attn_bv"), ("bd", "attn_bd"), ("gamma", "attn_gamma"), ("beta", "attn_beta"),
                   ("wr", "ffn_w_freq_real"), ("wi", "ffn_w_freq_imag"), ("fbias", "ffn_bias")):
        arrays[n] = np.ascontiguousarray(a[key])
    arrays["dft"], arrays["consts"], arrays["spread_f"] = dft, consts, spread_f

    nc = bacc.Bacc("TRN2", target_bir_lowering=False, num_devices=1)
    aps = {n: nc.dram_tensor(f"{n}_dram", v.shape, F32, kind="ExternalInput").ap() for n, v in arrays.items()}
    out = nc.dram_tensor("out_dram", x.shape, F32, kind="ExternalOutput").ap()
    build(nc, out=out, **aps)
    r = run_bass_kernel_spmd(nc, [{f"{n}_dram": v for n, v in arrays.items()}], core_ids=[0])
    return r.results[0]["out_dram"].reshape(8, 2048, 512)
```

```python
from contextlib import ExitStack

import concourse.bass as bass
from concourse import mybir

P = 128
TPG = 4
F32 = mybir.dt.float32
F32R = mybir.dt.float32r
I32 = mybir.dt.int32
U32 = mybir.dt.uint32
ALU = mybir.AluOpType
ACT = mybir.ActivationFunctionType
EPS_LN = 1e-5
EPS_INNER = 1e-12
EPS_ATTN = 1e-6
RSQRT_MAGIC = 1597463007
NEWTON = 3


def ticks(i, c):
    return c * 4 + (i - 3)


def two_back(i, c):
    return c * 4 - 4 if i < 2 else c * 4 + (i - 5)


def steps(b, i, c):
    return c * 4 + (i - 3) + b * 2


def back(i, c, n):
    return (i - n, c) if i >= n else (i - n + TPG, c - 1)


def wait(eng, sem, count):
    if isinstance(count, int) and count <= 0:
        return
    eng.wait_ge(sem, count + 1)


def wait_apart(eng, sem, value, settled, least):
    eng.wait_ge(settled, least)
    eng.wait_ge(sem, value + 1)


def build(nc, x, wq, wk, wv, wd, bq, bk, bv, bd, gamma, beta, wr, wi, fbias, dft, dft_mid, consts, spread_f, out):
    ROWS, D = x.shape
    C = D // P
    B = 8
    NG = ROWS // (B * P * TPG)
    NH = 16
    GR = TPG * P
    assert C == 4 and NG == 4 and D == 512 and GR == 512

    with ExitStack() as ctx:
        def sb(name, shape, dt=F32):
            return ctx.enter_context(nc.sbuf_tensor(name, shape, dt))

        def sem(name):
            return ctx.enter_context(nc.semaphore(name))

        def sems(name):
            return [sem(f"{name}{i}") for i in range(TPG)]

        q_T = sb("q_T", [P, C, NG * GR])
        w_qT = sb("w_qT", [P, 2, C, D], F32R)
        w_kT = sb("w_kT", [P, 2, C, D], F32R)
        w_m = sb("w_m", [P, 2, C, D], F32R)
        w_vT = sb("w_vT", [P, C, D])
        w_dT = sb("w_dT", [P, C, D])
        kvw = sb("kvw", [P, 2, C, D], F32R)
        act_T = sb("act_T", [P, 2, C, GR], F32R)
        x3_T = sb("x3_T", [P, 2, 2, C, P], F32R)
        xa = sb("xa", [P, TPG, D])
        xb = sb("xb", [P, TPG, D])
        x1f = sb("x1f", [P, TPG, D])
        x2 = sb("x2", [P, TPG, D])
        work = sb("work", [P, 8, D])
        k_acc = sb("k_acc", [P, D])
        kv_T = sb("kv_T", [P, C, P])
        ksum_h = sb("ksum_h", [P, C, NH])
        z_hl = sb("z_hl", [NH, 2, GR], F32R)
        gamma_bc = sb("gamma_bc", [P, D])
        beta_bc = sb("beta_bc", [P, D])
        bk1_bc = sb("bk1_bc", [P, D])
        bv_bc = sb("bv_bc", [P, D])
        bias_rows = sb("bias_rows", [P, D], F32R)
        cst = sb("cst", [P, 3 * P + C * NH])
        ident, head_mask, ones = cst[:, 0:P], cst[:, P:2 * P], cst[:, 2 * P:3 * P]
        own_head = cst[:, 3 * P:].rearrange("p (u h) -> p u h", h=NH)
        spread = sb("spread", [NH, C, P], F32R)
        pick = sb("pick", [P, 2, P], F32R)
        bq_col = sb("bq_col", [P, C])
        bq1_col = sb("bq1_col", [P, C])
        nbq_col = sb("nbq_col", [P, C])
        cols = sb("cols", [P, 2])
        eps_col = sb("eps_col", [P, 3])
        stats = sb("stats", [P, TPG, 6])
        mv1 = sb("mv1", [P, TPG, 2])
        r1 = sb("r1", [P, TPG])
        nm1 = sb("nm1", [P, TPG])
        nr = sb("nr", [P, 3, TPG])
        r1_all = sb("r1_all", [P, NG * TPG])
        r1_g = sb("r1_g", [P, TPG])
        bn = sb("bn", [P, 3, 6])
        mv = sb("mv", [P, 3, 2])
        sd = sb("sd", [P, 3])
        rs = sb("rs", [P, 3])
        nm = sb("nm", [P, 3])
        ssq = sb("ssq", [P, 2])
        sd_y = sb("sd_y", [P, 2])
        rs_y = sb("rs_y", [P, 2])

        k_hi, k_lo = kvw[:, 0, 0:2, :], kvw[:, 0, 2:4, :]
        x3_flat = x3_T[:].rearrange("p t s c n -> p t s (c n)")
        x1_hi = [kvw[:, 1, 0, :], kvw[:, 1, 1, :], x3_flat[:, 0, 0, :], x3_flat[:, 1, 0, :]]
        x1_lo = [kvw[:, 1, 2, :], kvw[:, 1, 3, :], x3_flat[:, 0, 1, :], x3_flat[:, 1, 1, :]]
        k1, e_k, k_f, e_q = (work[:, 2 * j:2 * j + 2, :] for j in range(4))
        h, x3 = (work[:, 2 * j:2 * j + 2, :] for j in range(2))
        junk = work[:, 5, :]
        den_sb = work[0:NH, 6, :]
        z_row = work[:, 4, :].rearrange("p (t n) -> p t n", t=TPG)
        kx_T = work[:, 0:4, :]
        cosm, sinm, w_cos, w_sin = (q_T[:, j, :].rearrange("p (c n) -> p c n", c=C) for j in range(4))
        s_T = work[:, 0:4, :]
        wr_sb, wi_sb = x2, xa
        half = D // 2

        banks = [ctx.enter_context(nc.psum_tensor(f"bank{i}", [P, D], F32)) for i in range(8)]
        kx_ps = banks[0:4]
        hs_ps = banks[0:2]
        den_ps, zrow_ps = banks[2], banks[3]
        zb_ps = [banks[3], banks[2]]
        kvw_banks = banks[0:2] + banks[4:6]
        mm_ps = banks[4:6]
        t_ps = banks[6:8]

        def setup_sems(names):
            return [sem(n) for n in names.split()]

        def made_by(names):
            return [sem(n) for n in names.split()]

        w_in, w_in2, w_in3, split_hi, split_done, pre, cols_ok, setup_done = setup_sems(
            "w_in w_in2 w_in3 split_hi split_done pre cols_ok setup_done")
        wr_in, wi_in, cos_in, sin_in, wvd_in, folded = setup_sems("wr_in wi_in cos_in sin_in wvd_in folded")
        m1_ps, m1_act, m2_ps, m2_c, m2_hi, m2_lo, m2_out = setup_sems("m1_ps m1_act m2_ps m2_c m2_hi m2_lo m2_out")
        xa_in, xb_in = sems("xa_in"), sems("xb_in")
        dve_ln1, ln1_bn = sem("dve_ln1"), sem("ln1_bn")

        by_sp = out_st = sems("out_st")
        by_pool = made_by("kacc_zero kacc_ok gam_ok gb_ok qlo_ok") + sems("x1lo_ok")
        kacc_zero, kacc_ok, gam_ok, gb_ok, qlo_ok = by_pool[:5]
        x1lo_ok = by_pool[5:]
        by_act = made_by("xthi rq_ok eq_ok rk_ok ek_ok khi_ok x1hi_ok kx_act kvwhi den_ok zhi_ok qhi_ok "
                         "sd_ok0 sd_ok1 sd_ok2 sdy_ok n_ok u_ok x3_ok x3hi ysq_ok") + sems("x1f_ok")
        xthi, rq_ok, eq_ok, rk_ok, ek_ok, khi_ok, x1hi_ok, kx_act, kvwhi, den_ok, zhi_ok, qhi_ok = by_act[:12]
        sd_ok, (sdy_ok, n_ok, u_ok, x3_ok, x3hi, ysq_ok), x1f_ok = by_act[12:15], by_act[15:21], by_act[21:]
        by_dve = made_by("ln1_ok xtlo q_ok k1_ok k_ok klo_ok ksum_ok kx_dve kv_ok kvwlo z_ok zlo_ok qp_ok r1g_ok h_ok "
                         "bn_ok0 bn_ok1 bn_ok2 mv_ok0 mv_ok1 mv_ok2 rs_ok nm_ok rsy_ok x3lo fin_ok") + sems("x2_ok")
        ln1_ok, xtlo, q_ok, k1_ok, k_ok, klo_ok, ksum_ok, kx_dve, kv_ok, kvwlo, z_ok, zlo_ok, qp_ok, r1g_ok, h_ok = by_dve[:15]
        bn_ok, mv_ok, (rs_ok, nm_ok, rsy_ok, x3lo, fin_ok), x2_ok = by_dve[15:18], by_dve[18:21], by_dve[21:26], by_dve[26:]
        by_pe = made_by("q_ps kx_done ksum_ps kv_ps kvw_ps d_ps dt_ps zt_ps zb_done hs_done x3t_ps y_ps") + sems("x1t_ps") + sems("k_ps")
        q_ps, kx_done, ksum_ps, kv_ps, kvw_ps, d_ps, dt_ps, zt_ps, zb_done, hs_done, x3t_ps, y_ps = by_pe[:12]
        x1t_ps, k_ps = by_pe[12:16], by_pe[16:]

        def start(eng, made):
            for one in made:
                eng.sem_inc(one, 1)

        chunked = lambda a: a.rearrange("(c p) n -> p c n", p=P)
        block = ctx.enter_context(nc.Block())

        @block.sync
        def _(sp):
            start(sp, by_sp)
            def load_xa(i, c, first_row):
                wait(sp, x1f_ok[i], c - 1)
                sp.dma_start(xa[:, i, :], x[bass.ds(first_row + i * P, P), :]).then_inc(xa_in[i], 16)

            def load_xb(i, c, first_row):
                wait(sp, x2_ok[i], c - 1)
                sp.dma_start(xb[:, i, :], x[bass.ds(first_row + i * P, P), :]).then_inc(xb_in[i], 16)

            def store(i, c, first_row):
                wait(sp, fin_ok, ticks(i, c))
                sp.dma_start(out[bass.ds(first_row + i * P, P), :], x2[:, i, :]).then_inc(out_st[i], 16)

            sp.dma_start(wr_sb[:], chunked(wr)).then_inc(wr_in, 16)
            sp.dma_start(cosm, chunked(dft[0])).then_inc(cos_in, 16)
            sp.dma_start(wi_sb[:], chunked(wi)).then_inc(wi_in, 16)
            sp.dma_start(sinm, chunked(dft[1])).then_inc(sin_in, 16)
            sp.dma_start(x1f[:], chunked(wq)).then_inc(w_in3, 16)
            sp.dma_start(cst[:], consts).then_inc(w_in, 16)
            sp.dma_start(k_acc[:], dft_mid).then_inc(w_in, 16)
            for dst, src in ((gamma_bc[:], gamma), (beta_bc[:], beta), (bk1_bc[:], bk), (bv_bc[:], bv)):
                sp.dma_start(dst, src.partition_broadcast(P)).then_inc(w_in2, 16)
            sp.dma_start(bq_col[:], bq).then_inc(w_in2, 16)
            sp.dma_start(den_sb, spread_f).then_inc(w_in2, 16)
            sp.dma_start(xb[:, 0, :], fbias.partition_broadcast(P)).then_inc(w_in2, 16)
            sp.dma_start(xb[:, 1, :], bd.partition_broadcast(P)).then_inc(w_in2, 16)
            sp.wait_ge(folded, 8)
            for i in range(TPG):
                load_xa(i, 1, 0)
            sp.wait_ge(split_done, 1)
            sp.dma_start(x1f[:], chunked(wk)).then_inc(w_in3, 16)
            sp.dma_start(w_vT[:], chunked(wv)).then_inc(wvd_in, 16)
            sp.dma_start(w_dT[:], chunked(wd)).then_inc(wvd_in, 16)
            for i in range(TPG):
                load_xa(i, 2, GR)
            sp.wait_ge(setup_done, 1)

            def batch(b, last):
                row = b * (NG * GR)
                for i in range(TPG):
                    load_xb(i, b * NG + 1, row)
                for g in range(2, NG + 2):
                    wrapped = last and g >= NG
                    for i in range(TPG):
                        load_xa(i, b * NG + (g + 1), 0 if wrapped else row + g * GR)
                for k in range(NG * TPG + TPG):
                    g, i = divmod(k, TPG)
                    if k >= TPG:
                        store(i, b * NG + g, row + (g - 1) * GR)
                    if g + 1 < NG:
                        load_xb(i, b * NG + (g + 2), row + (g + 1) * GR)

            with sp.Fori(0, B - 1) as b:
                batch(b, False)
            batch(B - 1, True)
            for i in range(TPG):
                wait(sp, out_st[i], 16 * B * NG)

        @block.gpsimd
        def _(pool):
            start(pool, by_pool)
            pool.memset(eps_col[:, 0:1], EPS_LN).then_inc(pre, 1)
            pool.memset(eps_col[:, 1:2], EPS_INNER).then_inc(pre, 1)
            pool.memset(eps_col[:, 2:3], 1.0).then_inc(pre, 1)

            def x1lo(i, c):
                wait(pool, x1hi_ok, ticks(i, c))
                pool.tensor_tensor(x1_lo[i], x1f[:, i, :], x1_hi[i], ALU.subtract).then_inc(x1lo_ok[i], 1)

            def kacc(i, c, b):
                wait(pool, k_ok, ticks(i, c))
                wait(pool, kacc_zero, b + 1)
                if i:
                    wait(pool, kacc_ok, ticks(i - 1, c))
                else:
                    wait(pool, kacc_ok, c * 4 - 4)
                pool.tensor_tensor(k_acc[:], k_acc[:], k_f[:, i % 2, :], ALU.add).then_inc(kacc_ok, 1)

            def affine(i, c):
                wait(pool, n_ok, ticks(i, c))
                pool.tensor_tensor(h[:, i % 2, :], h[:, i % 2, :], gamma_bc[:], ALU.mult).then_inc(gam_ok, 1)
                wait(pool, gam_ok, ticks(i, c))
                pool.tensor_tensor(h[:, i % 2, :], h[:, i % 2, :], beta_bc[:], ALU.add).then_inc(gb_ok, 1)

            def q_low(i, c, g):
                wait(pool, qhi_ok, ticks(i, c))
                s = slice(i * P, (i + 1) * P)
                pool.tensor_tensor(act_T[:, 1, :, s], q_T[:, :, bass.ds(g * GR + i * P, P)], act_T[:, 0, :, s],
                                   ALU.subtract).then_inc(qlo_ok, 1)

            pool.wait_ge(pre, 3)
            pool.wait_ge(setup_done, 1)
            with pool.Fori(0, B) as b:
                wait(pool, kv_ps, b)
                pool.tensor_tensor(cols[:], eps_col[:, 0:2], eps_col[:, 0:2], ALU.add)
                pool.memset(k_acc[:], 0.0).then_inc(kacc_zero, 1)
                with pool.Fori(0, NG) as g:
                    c = pool.snap(b * NG + g + 1)
                    for i in range(TPG):
                        x1lo(i, c)
                    for i in range(TPG):
                        kacc(i, c, b)
                c0 = pool.snap(b * NG + 1)
                for i in range(TPG):
                    q_low(i, c0, 0)
                for i in range(3):
                    affine(i, c0)
                q_low(0, c0 + 1, 1)
                affine(3, c0)
                with pool.Fori(1, NG - 1) as g:
                    c = pool.snap(b * NG + g + 1)
                    for i in range(3):
                        q_low(i + 1, c, g)
                        affine(i, c)
                    q_low(0, c + 1, g + 1)
                    affine(3, c)
                c3 = pool.snap(b * NG + NG)
                for i in range(3):
                    q_low(i + 1, c3, NG - 1)
                    affine(i, c3)
                affine(3, c3)
            for i in range(2):
                x1lo(i, B * NG + 1)

        @block.scalar
        def _(act):
            start(act, by_act)

            def copy(dst, src):
                return act.activation(dst, src, ACT.Copy)

            def make_x1f(i, c):
                wait(act, ln1_ok, c)
                wait(act, x1t_ps[i], c - 1)
                wait(act, x1lo_ok[i], c - 1)
                act.activation(x1f[:, i, :], xa[:, i, :], ACT.Identity, bias=nm1[:, i:i + 1], scale=r1[:, i:i + 1]).then_inc(x1f_ok[i], 1)

            def xt_hi(i, c):
                wait(act, x1t_ps[i], c)
                wait(act, k_ps[i], c - 1)
                copy(act_T[:, 0, :, i * P:(i + 1) * P], t_ps[i % 2][:].rearrange("p (c n) -> p c n", c=C)).then_inc(xthi, 1)

            def exp_q(u, c, q_banks=mm_ps * 2):
                wait(act, q_ps, ticks(u, c))
                wait(act, q_ok, two_back(u, c))
                act.activation(e_q[:, u % 2, :], q_banks[u][:], ACT.Relu, bias=nbq_col[:, u:u + 1], scale=-1.0).then_inc(rq_ok, 1)
                wait(act, rq_ok, ticks(u, c))
                act.activation(e_q[:, u % 2, :], e_q[:, u % 2, :], ACT.Exp, scale=-1.0).then_inc(eq_ok, 1)

            def split_x1(i, c, after_phase2=False):
                wait(act, kx_done, c * 4 - 4)
                if after_phase2:
                    wait(act, hs_done if i < 2 else y_ps, c * 4 - 4)
                wait(act, x1f_ok[i], c)
                copy(x1_hi[i], x1f[:, i, :]).then_inc(x1hi_ok, 1)

            def exp_k(i, c):
                wait(act, k1_ok, ticks(i, c))
                wait(act, k_ok, two_back(i, c))
                act.activation(e_k[:, i % 2, :], k1[:, i % 2, :], ACT.Relu, bias=eps_col[:, 2:3], scale=-1.0).then_inc(rk_ok, 1)
                wait(act, rk_ok, ticks(i, c))
                act.activation(e_k[:, i % 2, :], e_k[:, i % 2, :], ACT.Exp, scale=-1.0).then_inc(ek_ok, 1)

            def split_k(i, c):
                wait(act, k_ok, ticks(i, c))
                wait(act, kx_done, two_back(i, c))
                copy(k_hi[:, i % 2, :], k_f[:, i % 2, :]).then_inc(khi_ok, 1)

            def copy_den(c):
                wait(act, d_ps, c)
                wait(act, dt_ps, c - 1)
                copy(den_sb, den_ps[0:NH, :]).then_inc(den_ok, 1)

            def z_hi(c):
                wait(act, zt_ps, c)
                wait(act, zb_done, c * 4 - 4)
                copy(z_hl[:, 0, :], den_ps[0:NH, :]).then_inc(zhi_ok, 1)

            def q_hi(i, c, g, before):
                wait(act, qp_ok, c * 4)
                wait(act, hs_done, before)
                copy(act_T[:, 0, :, i * P:(i + 1) * P], q_T[:, :, bass.ds(g * GR + i * P, P)]).then_inc(qhi_ok, 1)

            def root(j, i, c):
                wait(act, mv_ok[j], ticks(i, c))
                eps = 0 if j else 1
                act.activation(sd[:, j:j + 1], mv[:, j, 1:2], ACT.Sqrt, bias=eps_col[:, eps:eps + 1]).then_inc(sd_ok[j], 1)

            def normalise(j, dst, src, done):
                act.activation(dst, src, ACT.Identity, bias=nm[:, j:j + 1], scale=rs[:, j:j + 1]).then_inc(done, 1)

            def make_n(i):
                normalise(0, h[:, i % 2, :], h[:, i % 2, :], n_ok)

            def make_u(i):
                normalise(1, h[:, i % 2, :], h[:, i % 2, :], u_ok)

            def make_x3(i, c):
                wait(act, x3t_ps, two_back(i, c))
                normalise(2, x3[:, i % 2, :], x2[:, i, :], x3_ok)

            def x3_hi(i, c):
                wait(act, x3t_ps, ticks(i, c))
                wait(act, y_ps, two_back(i, c))
                copy(x3_T[:, i % 2, 0, :, :], t_ps[i % 2][:].rearrange("p (c n) -> p c n", c=C)).then_inc(x3hi, 1)

            def y_root(i, c):
                wait(act, y_ps, ticks(i, c))
                act.activation(junk, mm_ps[i % 2][:], ACT.Square, accum_out=ssq[:, i % 2:i % 2 + 1]).then_inc(ysq_ok, 1)
                wait(act, ysq_ok, ticks(i, c))
                act.activation(sd_y[:, i % 2:i % 2 + 1], ssq[:, i % 2:i % 2 + 1], ACT.Sqrt, bias=eps_col[:, 0:1], scale=1.0 / D).then_inc(sdy_ok, 1)

            act.wait_ge(pre, 3)

            def left_half(n):
                act.wait_ge(m1_ps, n + 1)
                copy(s_T[:, n, :], banks[n][:]).then_inc(m1_act, 1)

            def m_hi(n):
                act.wait_ge(m2_c, n + 1)
                copy(w_m[:, 0, n, :], work[:, 4 + n, :]).then_inc(m2_hi, 1)

            act.wait_ge(w_in3, 16)
            copy(w_qT[:, 0], x1f[:]).then_inc(split_hi, 1)
            left_half(0)
            left_half(1)
            act.wait_ge(w_in3, 32)
            copy(w_kT[:, 0], x1f[:]).then_inc(split_hi, 1)
            left_half(2)
            left_half(3)
            act.wait_ge(split_done, 2)
            for i in range(TPG):
                make_x1f(i, 1)
            m_hi(0)
            for i in range(TPG):
                xt_hi(i, 1)
            for n in range(1, C):
                m_hi(n)
            for i in range(2):
                split_x1(i, 1)
            for i in range(2):
                make_x1f(i, 2)
            act.wait_ge(setup_done, 1)

            def phase1(c, more, first=False):
                q_banks = banks[0:4] if first else mm_ps * 2
                exp_q(0, c, q_banks)
                exp_q(1, c, q_banks)
                if first:
                    split_x1(2, c, True)
                    split_x1(3, c, True)
                    exp_q(2, c, q_banks)
                    exp_q(3, c, q_banks)
                    make_x1f(2, c + 1)
                    make_x1f(3, c + 1)
                else:
                    split_x1(0, c)
                    split_x1(1, c)
                    exp_q(2, c)
                    split_x1(2, c)
                    split_x1(3, c)
                    exp_q(3, c)
                    make_x1f(0, c + 1)
                    make_x1f(1, c + 1)
                for i in range(TPG):
                    exp_k(i, c)
                    if i < 2 and not first:
                        make_x1f(i + 2, c + 1)
                    if more:
                        xt_hi(i, c + 1)
                    split_k(i, c)

            def slot(i, c, b, prev, coming=None, den=None, more=True):
                one, two, three, four = (back(i, c, n) if prev or i >= n else None for n in (1, 2, 3, 4))
                if coming is not None:
                    q_hi(*coming)
                if den is not None:
                    copy_den(den)
                if not more:
                    wait(act, hs_done, ticks(i, c))
                    xt_hi(i, c + 1)
                if two:
                    root(2, *two)
                if three and more:
                    x3_hi(*three)
                root(0, i, c)
                if one:
                    root(1, *one)
                if four:
                    y_root(*four)
                wait(act, nm_ok, steps(b, i, c))
                make_n(i)
                if three and not more:
                    x3_hi(*three)
                if den is not None:
                    z_hi(den)
                if one:
                    make_u(one[0])
                if two:
                    make_x3(*two)

            def phase2(c, b, g, prev, more):
                done = c * 4 - 4
                coming = [(1, c, g, done), (2, c, g, done), (3, c, g, done), (0, c + 1, g + 1, c * 4 - 3) if more else None]
                turned = 0 if prev else 1
                for i in range(TPG):
                    slot(i, c, b, prev, coming[i] if prev else None, c + 1 if more and i == turned else None, more)
                if not prev:
                    q_hi(*coming[3])

            def phase2_end(c, b):
                root(2, 2, c)
                root(1, 3, c)
                wait(act, nm_ok, steps(b, 0, c + 1))
                make_u(3)
                make_x3(2, c)
                x3_hi(1, c)
                root(2, 3, c)
                wait(act, nm_ok, steps(b, 1, c + 1))
                make_x3(3, c)
                split_x1(0, c + 1, True)
                split_x1(1, c + 1, True)
                y_root(0, c)
                x3_hi(2, c)
                y_root(1, c)
                x3_hi(3, c)
                y_root(2, c)
                make_x1f(0, c + 2)
                y_root(3, c)
                make_x1f(1, c + 2)

            with act.Fori(0, B) as b:
                phase1(act.snap(b * NG + 1), True, True)
                with act.Fori(1, NG - 1) as g:
                    phase1(act.snap(b * NG + g + 1), True)
                c3 = act.snap(b * NG + NG)
                phase1(c3, False)
                wait(act, kx_done, c3 * 4)
                for j in (2, 0):
                    copy(kx_T[:, j, :], kx_ps[j][:]).then_inc(kx_act, 1)
                c0 = act.snap(b * NG + 1)
                copy_den(c0)
                z_hi(c0)
                for u in range(C):
                    if u == 3:
                        q_hi(0, c0, 0, c0 * 4 - 4)
                    wait(act, kvw_ps, b * C + (u + 1))
                    copy(kvw[:, 0, u, :], kvw_banks[u][:]).then_inc(kvwhi, 1)
                for i in range(1, TPG):
                    q_hi(i, c0, 0, c0 * 4 - 4)
                phase2(c0, b, 0, False, True)
                with act.Fori(1, NG - 1) as g:
                    phase2(act.snap(b * NG + g + 1), b, g, True, True)
                c3 = act.snap(b * NG + NG)
                phase2(c3, b, NG - 1, True, False)
                phase2_end(c3, b)

        @block.vector
        def _(dve):
            start(dve, by_dve)
            def fold(even, odd, w, minus):
                low, high = w[:, :, 1:half], w[:, :, half + 1:]
                dve.tensor_copy(even[:, :, 0:1], w[:, :, 0:1]).then_inc(folded, 1)
                dve.tensor_tensor(even[:, :, 1:half], low, high, ALU.add).then_inc(folded, 1)
                dve.tensor_copy(even[:, :, half:half + 1], w[:, :, half:half + 1]).then_inc(folded, 1)
                odd_of = (high, low) if minus else (low, high)
                dve.tensor_tensor(odd[:, :, half + 1:], odd_of[0], odd_of[1], ALU.subtract).then_inc(folded, 1)

            dve.wait_ge(wr_in, 16)
            fold(w_cos, w_sin, wr_sb, False)
            dve.wait_ge(wi_in, 16)
            fold(w_sin, w_cos, wi_sb, True)
            dve.wait_ge(split_hi, 1)
            dve.tensor_tensor(w_qT[:, 1], x1f[:], w_qT[:, 0], ALU.subtract).then_inc(split_done, 1)

            setup_steps = [0]

            def link(ins):
                setup_steps[0] += 1
                ins.then_inc(m2_out, 1)
                dve.wait_ge(m2_out, setup_steps[0])

            def centre(dst, src, scale):
                link(dve.bn_stats(bn[:, 0, :], src))
                link(dve.bn_aggr(mv[:, 0, :], bn[:, 0, :]))
                return dve.tensor_scalar(dst, src, mv[:, 0, 0:1], scale, ALU.subtract, ALU.mult)

            def m_rows(n):
                dve.wait_ge(m2_ps, n + 1)
                centre(work[:, 4 + n, :], banks[4 + n % 2][:], 1.0 / D).then_inc(m2_c, 1)
                dve.wait_ge(m2_hi, n + 1)
                dve.tensor_tensor(w_m[:, 1, n, :], work[:, 4 + n, :], w_m[:, 0, n, :], ALU.subtract).then_inc(setup_done if n == C - 1 else m2_lo, 1)

            def small_ones():
                dve.wait_ge(w_in2, 16 * 8)
                dve.tensor_scalar(bk1_bc[:], bk1_bc[:], 1.0, None, ALU.add)
                dve.tensor_scalar(bq1_col[:], bq_col[:], 1.0, None, ALU.add)
                dve.tensor_scalar(nbq_col[:], bq_col[:], -1.0, None, ALU.mult)
                dve.wait_ge(w_in, 16 * 2)
                dve.tensor_tensor(cols[:, 0:1], ident[:, 0:1], ident[:, 1:2], ALU.add)
                dve.tensor_tensor(cols[:, 1:2], ident[:, 2:3], ident[:, 3:4], ALU.add).then_inc(cols_ok, 1)
                dve.wait_ge(cols_ok, 1)
                for n in range(2):
                    dve.tensor_scalar(pick[:, n, :], ones, cols[:, n:n + 1], None, ALU.mult)
                link(dve.tensor_copy(spread[:], den_sb.rearrange("h (u n) -> h u n", u=C)))

            def bias_parts():
                fb, bd_b, acc, hi_f = (xb[:, n, :] for n in range(4))
                link(centre(fb, fb, 1.0))
                link(dve.memset(acc, 0.0))
                for n, bias in enumerate((fb, bd_b)):
                    link(dve.tensor_copy(bias_rows[:], bias))
                    link(dve.tensor_copy(hi_f, bias_rows[:]))
                    link(dve.tensor_tensor(bias, bias, hi_f, ALU.subtract))
                    for part, row in ((hi_f, 2 * n), (bias, 2 * n + 1)):
                        link(dve.scalar_tensor_tensor(out=acc, in0=part, scalar=ident[:, row:row + 1], in1=acc, op0=ALU.mult, op1=ALU.add))
                link(dve.tensor_copy(bias_rows[:], acc))

            def ln1_stats(i, c):
                dve.wait_ge(xa_in[i], c * 16)
                dve.bn_stats(stats[:, i, :], xa[:, i, :]).then_inc(ln1_bn, 1)

            LN1_STEPS = 2 + 3 * NEWTON + 2

            def ln1_finish(c, g=None):
                n = [0]

                def step(ins):
                    n[0] += 1
                    ins.then_inc(dve_ln1, 1)
                    dve.wait_ge(dve_ln1, (c - 1) * LN1_STEPS + n[0])

                dve.wait_ge(ln1_bn, c * 4)
                if g is not None:
                    dve.tensor_copy(r1_all[:, bass.ds(g * TPG, TPG)], r1[:])
                for i in range(TPG):
                    ins = dve.bn_aggr(mv1[:, i, :], stats[:, i, :])
                step(ins)
                v, y, a = nr[:, 0, :], nr[:, 1, :], nr[:, 2, :]
                step(dve.tensor_scalar(v, mv1[:, :, 1], EPS_LN, None, ALU.add))
                step(dve.tensor_scalar(a.bitcast(U32), v.bitcast(U32), 1, None, ALU.logical_shift_right))
                wait(dve, x1f_ok[3], c - 1)
                step(dve.tensor_scalar(y.bitcast(I32), a.bitcast(I32), -1, RSQRT_MAGIC, ALU.mult, ALU.add))
                for s in range(NEWTON):
                    step(dve.scalar_tensor_tensor(out=a, in0=y, scalar=-0.5, in1=v, op0=ALU.mult, op1=ALU.mult))
                    step(dve.tensor_tensor(a, a, y, ALU.mult))
                    last = s == NEWTON - 1
                    step(dve.scalar_tensor_tensor(out=r1[:] if last else y, in0=a, scalar=1.5, in1=y, op0=ALU.add, op1=ALU.mult))
                assert n[0] == LN1_STEPS
                dve.scalar_tensor_tensor(out=nm1[:], in0=mv1[:, :, 0], scalar=-1.0, in1=r1[:], op0=ALU.mult,
                                         op1=ALU.mult).then_inc(ln1_ok, 1)

            def xt_lo(i, c):
                wait(dve, xthi, ticks(i, c))
                s = slice(i * P, (i + 1) * P)
                dve.tensor_tensor(act_T[:, 1, :, s], t_ps[i % 2][:].rearrange("p (c n) -> p c n", c=C),
                                  act_T[:, 0, :, s], ALU.subtract).then_inc(xtlo, 1)

            def q_feature(u, c, g, q_banks=mm_ps * 2):
                wait(dve, eq_ok, ticks(u, c))
                dve.scalar_tensor_tensor(out=q_T[:, u, bass.ds(g * GR, GR)], in0=q_banks[u][:], scalar=bq1_col[:, u:u + 1],
                                         in1=e_q[:, u % 2, :], op0=ALU.add, op1=ALU.max).then_inc(q_ok, 1)

            def k_bias(i, c):
                wait(dve, k_ps[i], c)
                wait(dve, ek_ok, two_back(i, c))
                dve.tensor_tensor(k1[:, i % 2, :], mm_ps[i % 2][:], bk1_bc[:], ALU.add).then_inc(k1_ok, 1)

            def k_feature(i, c):
                wait(dve, ek_ok, ticks(i, c))
                wait(dve, kacc_ok, two_back(i, c))
                wait(dve, khi_ok, two_back(i, c))
                dve.tensor_tensor(k_f[:, i % 2, :], e_k[:, i % 2, :], k1[:, i % 2, :], ALU.max).then_inc(k_ok, 1)

            def k_low(i, c):
                wait(dve, khi_ok, ticks(i, c))
                dve.tensor_tensor(k_lo[:, i % 2, :], k_f[:, i % 2, :], k_hi[:, i % 2, :], ALU.subtract).then_inc(klo_ok, 1)

            def phase1(c, g, more, first=False):
                if first:
                    for u in range(C):
                        q_feature(u, c, g, banks[0:4])
                        if u == 1:
                            k_bias(0, c)
                else:
                    for i in range(TPG):
                        ln1_stats(i, c + 1)
                    q_feature(0, c, g)
                    ln1_finish(c + 1, g)
                    for u in range(1, C):
                        q_feature(u, c, g)
                    k_bias(0, c)
                for i in range(TPG):
                    k_feature(i, c)
                    if more:
                        xt_lo(i, c + 1)
                    if i + 1 < TPG:
                        k_bias(i + 1, c)
                    k_low(i, c)

            def invert(c):
                wait(dve, dt_ps, c)
                wait(dve, zt_ps, c - 1)
                dve.reciprocal(z_row[:, :, 0:NH], zrow_ps[:, 0:TPG * NH].rearrange("p (t h) -> p t h", h=NH)).then_inc(z_ok, 1)

            def z_low(c):
                wait(dve, zhi_ok, c)
                dve.tensor_tensor(z_hl[:, 1, :], den_ps[0:NH, :], z_hl[:, 0, :], ALU.subtract).then_inc(zlo_ok, 1)

            def q_scaled(u, c, g):
                wait(dve, zb_done, ticks(u, c))
                rows = bass.ds(g * GR, GR)
                dve.tensor_tensor(q_T[:, u, rows], zb_ps[u % 2][:], q_T[:, u, rows], ALU.mult).then_inc(qp_ok, 1)

            def residual(i, c):
                wait(dve, hs_done, ticks(i, c))
                dve.wait_ge(xb_in[i], c * 16)
                wait(dve, r1g_ok, c)
                dve.scalar_tensor_tensor(out=h[:, i % 2, :], in0=xb[:, i, :], scalar=r1_g[:, i:i + 1], in1=hs_ps[i % 2][:],
                                         op0=ALU.mult, op1=ALU.add).then_inc(h_ok, 1)

            def stats_of(j, src):
                dve.bn_stats(bn[:, j, :], src).then_inc(bn_ok[j], 1)

            def moments(j, i, c):
                wait_apart(dve, bn_ok[j], ticks(i, c), pre, 3)
                dve.bn_aggr(mv[:, j, :], bn[:, j, :]).then_inc(mv_ok[j], 1)

            def scales(first, end, root_of, tile, step):
                wait(dve, sd_ok[root_of], tile)
                dve.reciprocal(rs[:, first:end], sd[:, first:end]).then_inc(rs_ok, 1)
                wait(dve, rs_ok, step)
                dve.scalar_tensor_tensor(out=nm[:, first:end], in0=mv[:, first:end, 0], scalar=-1.0, in1=rs[:, first:end],
                                         op0=ALU.mult, op1=ALU.mult).then_inc(nm_ok, 1)

            def add_x(i, c):
                wait(dve, u_ok, ticks(i, c))
                wait(dve, out_st[i], c * 16 - 16)
                dve.tensor_tensor(x2[:, i, :], xb[:, i, :], h[:, i % 2, :], ALU.add).then_inc(x2_ok[i], 1)

            def x3_low(i, c):
                wait(dve, x3hi, ticks(i, c))
                dve.tensor_tensor(x3_T[:, i % 2, 1, :, :], t_ps[i % 2][:].rearrange("p (c n) -> p c n", c=C),
                                  x3_T[:, i % 2, 0, :, :], ALU.subtract).then_inc(x3lo, 1)

            def finish(i, c):
                wait(dve, sdy_ok, ticks(i, c))
                dve.reciprocal(rs_y[:, i % 2:i % 2 + 1], sd_y[:, i % 2:i % 2 + 1]).then_inc(rsy_ok, 1)
                wait(dve, rsy_ok, ticks(i, c))
                dve.scalar_tensor_tensor(out=x2[:, i, :], in0=mm_ps[i % 2][:], scalar=rs_y[:, i % 2:i % 2 + 1],
                                         in1=x2[:, i, :], op0=ALU.mult, op1=ALU.add).then_inc(fin_ok, 1)

            def stats_u(i, c):
                wait(dve, gb_ok, ticks(i, c))
                stats_of(1, h[:, i % 2, :])

            def stats_x2(i, c):
                wait(dve, x2_ok[i], c)
                stats_of(2, x2[:, i, :])

            def slot(i, c, b, prev, z=None, scaled=(), more=True):
                one, two, three, four = (back(i, c, n) if prev or i >= n else None for n in (1, 2, 3, 4))
                if two:
                    add_x(*two)
                    wait(dve, x2_ok[two[0]], two[1])
                residual(i, c)
                if two:
                    stats_of(2, x2[:, two[0], :])
                if not more:
                    xt_lo(i, c + 1)
                wait(dve, h_ok, ticks(i, c))
                stats_of(0, h[:, i % 2, :])
                if not prev:
                    for q in scaled:
                        q_scaled(*q)
                if one:
                    stats_u(*one)
                if two:
                    moments(2, *two)
                moments(0, i, c)
                if one:
                    moments(1, *one)
                if z is not None:
                    invert(z)
                if three and more:
                    x3_low(*three)
                if one:
                    scales(0, 3 if two else 2, 1, ticks(*one), steps(b, i, c))
                else:
                    scales(0, 1, 0, ticks(i, c), steps(b, i, c))
                if prev:
                    for q in scaled:
                        q_scaled(*q)
                if four:
                    finish(*four)
                if three and not more:
                    x3_low(*three)

            def phase2(c, b, g, prev, more):
                dve.tensor_copy(r1_g[:], r1_all[:, bass.ds(g * TPG, TPG)]).then_inc(r1g_ok, 1)
                turned = 0 if prev else 1
                for i in range(TPG):
                    n = i - turned - 1
                    slot(i, c, b, prev, c + 1 if more and i == turned else None,
                         [(u, c + 1, g + 1) for u in (2 * n, 2 * n + 1)] if more and n in (0, 1) else (), more)
                    if more and i == turned:
                        z_low(c + 1)

            def phase2_end(c, b):
                add_x(2, c)
                stats_x2(2, c)
                stats_u(3, c)
                moments(2, 2, c)
                moments(1, 3, c)
                scales(1, 3, 1, ticks(3, c), steps(b, 0, c + 1))
                for i in range(2):
                    ln1_stats(i, c + 2)
                x3_low(1, c)
                add_x(3, c)
                stats_x2(3, c)
                moments(2, 3, c)
                ln1_stats(2, c + 2)
                scales(2, 3, 2, ticks(3, c), steps(b, 1, c + 1))
                ln1_stats(3, c + 2)
                finish(0, c)
                x3_low(2, c)
                finish(1, c)
                x3_low(3, c)
                ln1_finish(c + 2, 0)
                finish(2, c)
                finish(3, c)

            small_ones()
            bias_parts()
            for i in range(TPG):
                ln1_stats(i, 1)
            ln1_finish(1)
            dve.wait_ge(split_hi, 2)
            dve.tensor_tensor(w_kT[:, 1], x1f[:], w_kT[:, 0], ALU.subtract).then_inc(split_done, 1)
            m_rows(0)
            for i in range(TPG):
                xt_lo(i, 1)
            m_rows(1)
            m_rows(2)
            for i in range(TPG):
                ln1_stats(i, 2)
            ln1_finish(2, 0)
            dve.wait_ge(wvd_in, 32)
            m_rows(3)

            with dve.Fori(0, B) as b:
                phase1(dve.snap(b * NG + 1), 0, True, True)
                with dve.Fori(1, NG - 1) as g:
                    phase1(dve.snap(b * NG + g + 1), g, True)
                c3 = dve.snap(b * NG + NG)
                phase1(c3, NG - 1, False)
                wait(dve, ksum_ps, b + 1)
                dve.scalar_tensor_tensor(out=ksum_h[:], in0=t_ps[1][:, 0:C * NH].rearrange("p (u h) -> p u h", h=NH), scalar=EPS_ATTN,
                                         in1=own_head, op0=ALU.add, op1=ALU.mult).then_inc(ksum_ok, 1)
                wait(dve, kx_done, c3 * 4)
                for j in (1, 3):
                    dve.tensor_copy(kx_T[:, j, :], kx_ps[j][:]).then_inc(kx_dve, 1)
                mask4 = head_mask.unsqueeze(1).broadcast_to([P, C, P])
                c0 = dve.snap(b * NG + 1)
                invert(c0)
                z_low(c0)
                wait(dve, kv_ps, b + 1)
                dve.tensor_tensor(kv_T[:], t_ps[0][:].rearrange("p (c n) -> p c n", c=C), mask4, ALU.mult).then_inc(kv_ok, 1)
                for u in range(C):
                    if u < 2:
                        q_scaled(2 * u, c0, 0)
                        q_scaled(2 * u + 1, c0, 0)
                    wait(dve, kvwhi, b * C + (u + 1))
                    dve.tensor_tensor(kvw[:, 1, u, :], kvw_banks[u][:], kvw[:, 0, u, :], ALU.subtract).then_inc(kvwlo, 1)
                phase2(c0, b, 0, False, True)
                with dve.Fori(1, NG - 1) as g:
                    phase2(dve.snap(b * NG + g + 1), b, g, True, True)
                c3 = dve.snap(b * NG + NG)
                phase2(c3, b, NG - 1, True, False)
                phase2_end(c3, b)

        @block.tensor
        def _(pe):
            start(pe, by_pe)

            def split_product(dst, left_hi, left_lo, right_hi, right_lo, start, stop, **kw):
                pe.matmul(dst, left_hi, right_hi, start=start, stop=False, **kw)
                pe.matmul(dst, left_hi, right_lo, start=False, stop=False, **kw)
                return pe.matmul(dst, left_lo, right_hi, start=False, stop=stop, **kw)

            for n in range(C):
                o = slice(n * P, (n + 1) * P)
                for part, (left, right) in enumerate(((w_cos, cosm), (w_sin, sinm))):
                    if n == 0:
                        pe.wait_ge((cos_in, sin_in)[part], 16)
                        pe.wait_ge(folded, 2 + 4 * part)
                    elif n == 2:
                        pe.wait_ge(folded, 8)
                    for j in range(C):
                        mm = pe.matmul(banks[n][:], left[:, j, o], right[:, j, :], start=(part == 0 and j == 0),
                                       stop=(part == 1 and j == C - 1))
                mm.then_inc(m1_ps, 1)
            pe.wait_ge(w_in, 16 * 2)
            right_half = (cosm[:, 0, :], cosm[:, 1, :], k_acc[:], sinm[:, 1, :])

            def m_product(n):
                o = slice(n * P, (n + 1) * P)
                if n >= 2:
                    pe.wait_ge(m2_c, n - 1)
                for j in range(C):
                    if n == 0:
                        pe.wait_ge(m1_act, j + 1)
                    mm = pe.matmul(banks[4 + n % 2][:], s_T[:, j, o], right_half[j], start=(j == 0), stop=(j == C - 1))
                mm.then_inc(m2_ps, 1)

            def transpose_x1(i, c):
                wait(pe, x1f_ok[i], c)
                wait(pe, xtlo, two_back(i, c))
                for j in range(C):
                    mm = pe.transpose(t_ps[i % 2][:, j * P:(j + 1) * P], x1f[:, i, j * P:(j + 1) * P], ident)
                mm.then_inc(x1t_ps[i], 1)

            def project_q(u, c, first=False):
                wait(pe, xtlo, c * 4)
                if first:
                    wait(pe, h_ok, c * 4 - 4)
                    wait(pe, qp_ok, c * 4 - 4)
                elif u < 2:
                    wait(pe, k1_ok, c * 4 - 4)
                else:
                    wait(pe, q_ok, ticks(u - 2, c))
                for j in range(C):
                    o = slice(u * P, (u + 1) * P)
                    mm = split_product((banks[u] if first else mm_ps[u % 2])[:], w_qT[:, 0, j, o], w_qT[:, 1, j, o], act_T[:, 0, j, :], act_T[:, 1, j, :],
                                       j == 0, j == C - 1)
                mm.then_inc(q_ps, 1)

            def project_k(i, c, first):
                if i < 2 and first:
                    wait(pe, k1_ok, c * 4 - 4)
                    wait(pe, fin_ok, c * 4 - 5 + i)
                elif i < 2:
                    wait(pe, q_ok, ticks(i + 2, c))
                else:
                    wait(pe, k1_ok, ticks(i - 2, c))
                for j in range(C):
                    s = slice(i * P, (i + 1) * P)
                    mm = split_product(mm_ps[i % 2][:], act_T[:, 0, j, s], act_T[:, 1, j, s], w_kT[:, 0, j, :], w_kT[:, 1, j, :],
                                       j == 0, j == C - 1)
                mm.then_inc(k_ps[i], 1)

            def outer_kx(i, c, first):
                wait(pe, x1lo_ok[i], c)
                wait(pe, klo_ok, ticks(i, c))
                if first:
                    wait(pe, q_ok, c * 4)
                for j in range(C):
                    o = slice(j * P, (j + 1) * P)
                    mm = split_product(kx_ps[j][:], x1_hi[i][:, o], x1_lo[i][:, o], k_hi[:, i % 2, :], k_lo[:, i % 2, :],
                                       first, False, skip_group_check=True)
                mm.then_inc(kx_done, 1)

            def phase1(c, first, more):
                if not first:
                    project_q(0, c)
                    outer_kx(2, c - 1, False)
                    project_q(1, c)
                    outer_kx(3, c - 1, False)
                    project_q(2, c)
                    project_q(3, c)
                project_k(0, c, first)
                if more:
                    transpose_x1(0, c + 1)
                project_k(1, c, first)
                if more:
                    transpose_x1(1, c + 1)
                project_k(2, c, first)
                if more:
                    transpose_x1(2, c + 1)
                outer_kx(0, c, first)
                project_k(3, c, first)
                if more:
                    transpose_x1(3, c + 1)
                outer_kx(1, c, False)

            def denominators(c, g):
                wait(pe, qp_ok, c * 4 - 4)
                for u in range(C):
                    mm = pe.matmul(den_ps[0:NH, :], ksum_h[:, u, :], q_T[:, u, bass.ds(g * GR, GR)], start=(u == 0), stop=(u == C - 1))
                mm.then_inc(d_ps, 1)

            def turn_denominators(c):
                wait(pe, den_ok, c)
                pe.matmul(zrow_ps[:, 0:NH], ident, ones[:, 0:NH], start=True, stop=True)
                for t in range(TPG):
                    mm = pe.transpose(zrow_ps[:, t * NH:(t + 1) * NH], den_sb[:, t * P:(t + 1) * P], ident[0:NH, 0:NH])
                mm.then_inc(dt_ps, 1)

            def turn_back(c):
                wait(pe, z_ok, c)
                for t in range(TPG):
                    mm = pe.transpose(den_ps[:, t * P:(t + 1) * P], z_row[:, t, :], ident)
                mm.then_inc(zt_ps, 1)

            def spread_z(u, c):
                wait(pe, zlo_ok, c)
                if u >= 2:
                    wait(pe, qp_ok, ticks(u - 2, c))
                pe.matmul(zb_ps[u % 2][:], spread[:, u, :], z_hl[:, 0, :], start=True, stop=False)
                pe.matmul(zb_ps[u % 2][:], spread[:, u, :], z_hl[:, 1, :], start=False, stop=True).then_inc(zb_done, 1)

            def attention(i, c):
                wait(pe, qlo_ok, ticks(i, c))
                wait(pe, h_ok, two_back(i, c))
                pe.matmul(hs_ps[i % 2][:], pick[:, 1, :], bias_rows[:], start=True, stop=False)
                for u in range(C):
                    s = slice(i * P, (i + 1) * P)
                    mm = split_product(hs_ps[i % 2][:], act_T[:, 0, u, s], act_T[:, 1, u, s], kvw[:, 0, u, :], kvw[:, 1, u, :],
                                       False, u == C - 1)
                mm.then_inc(hs_done, 1)

            def transpose_x3(i, c):
                wait(pe, x3_ok, ticks(i, c))
                wait(pe, x3lo, two_back(i, c))
                for j in range(C):
                    mm = pe.transpose(t_ps[i % 2][:, j * P:(j + 1) * P], x3[:, i % 2, j * P:(j + 1) * P], ident)
                mm.then_inc(x3t_ps, 1)

            def ffn(i, c):
                wait(pe, x3lo, ticks(i, c))
                wait(pe, fin_ok, two_back(i, c))
                pe.matmul(mm_ps[i % 2][:], pick[:, 0, :], bias_rows[:], start=True, stop=False)
                for j in range(C):
                    mm = split_product(mm_ps[i % 2][:], x3_T[:, i % 2, 0, j, :], x3_T[:, i % 2, 1, j, :], w_m[:, 0, j, :], w_m[:, 1, j, :],
                                       False, j == C - 1)
                mm.then_inc(y_ps, 1)

            def phase2(c, g, prev, more):
                if more and prev:
                    denominators(c + 1, g + 1)
                turned = 0 if prev else 1
                for i in range(TPG):
                    attention(i, c)
                    n = i - turned - 1
                    if more and i == turned:
                        if not prev:
                            denominators(c + 1, g + 1)
                        turn_denominators(c + 1)
                    if more and n in (0, 1):
                        spread_z(2 * n, c + 1)
                        spread_z(2 * n + 1, c + 1)
                    if not more:
                        wait(pe, x3lo, ticks(i, c) - 4)
                        transpose_x1(i, c + 1)
                        ffn(i, c - 1)
                        if i:
                            wait(pe, xtlo, ticks(i - 1, c + 1))
                    if prev or i == 3:
                        transpose_x3(*back(i, c, 3))
                    if prev and more:
                        ffn(i, c - 1)
                    if more and i == turned:
                        turn_back(c + 1)

            def phase2_end(c):
                project_q(0, c + 1, True)
                transpose_x3(1, c)
                ffn(0, c)
                transpose_x3(2, c)
                project_q(1, c + 1, True)
                ffn(1, c)
                transpose_x3(3, c)
                ffn(2, c)
                ffn(3, c)
                project_q(2, c + 1, True)
                project_q(3, c + 1, True)

            m_product(0)
            m_product(1)
            for i in range(TPG):
                transpose_x1(i, 1)
            m_product(2)
            m_product(3)
            pe.wait_ge(split_done, 2)
            for u in range(C):
                project_q(u, 1, True)
            pe.wait_ge(setup_done, 1)

            with pe.Fori(0, B) as b:
                phase1(pe.snap(b * NG + 1), True, True)
                with pe.Fori(1, NG - 1) as g:
                    phase1(pe.snap(b * NG + g + 1), False, True)
                c3 = pe.snap(b * NG + NG)
                phase1(c3, False, False)

                outer_kx(2, c3, False)
                wait(pe, kacc_ok, c3 * 4)
                wait(pe, xtlo, c3 * 4)
                for u in range(C):
                    mm = pe.matmul(t_ps[1][:, u * NH:(u + 1) * NH], k_acc[:, u * P:(u + 1) * P], ones[:, 0:NH], start=True, stop=True)
                mm.then_inc(ksum_ps, 1)
                outer_kx(3, c3, False)
                wait(pe, kx_act, b * 2 + 1)
                wait(pe, ksum_ok, b + 1)
                c0 = pe.snap(b * NG + 1)
                denominators(c0, 0)
                wait(pe, kx_act, b * 2 + 2)
                wait(pe, kx_dve, b * 2 + 2)
                for u in range(C):
                    if u == 1:
                        turn_denominators(c0)
                    if u == 2:
                        turn_back(c0)
                    o = slice(u * P, (u + 1) * P)
                    for j in range(C):
                        pe.matmul(t_ps[0][:, o], w_vT[:, j, o], kx_T[:, j, o], start=(j == 0), stop=False)
                    mm = pe.matmul(t_ps[0][:, o], bv_bc[:, o], k_acc[:, o], start=False, stop=True)
                mm.then_inc(kv_ps, 1)
                spread_z(0, c0)
                spread_z(1, c0)
                wait(pe, kv_ok, b + 1)
                for u in range(C):
                    if u == 2:
                        spread_z(2, c0)
                        spread_z(3, c0)
                    pe.matmul(kvw_banks[u][:], kv_T[:, u, :], w_dT[:, u, :], start=True, stop=True).then_inc(kvw_ps, 1)
                wait(pe, kvwlo, b * C + C)
                phase2(c0, 0, False, True)
                with pe.Fori(1, NG - 1) as g:
                    phase2(pe.snap(b * NG + g + 1), g, True, True)
                c3 = pe.snap(b * NG + NG)
                phase2(c3, NG - 1, True, False)
                phase2_end(c3)


def constants():
    import numpy as np
    d = 512
    jk = np.outer(np.arange(d), np.arange(d)) % d
    cos, sin = np.cos(2 * np.pi * jk / d), np.sin(2 * np.pi * jk / d)
    dft = np.stack([cos, sin]).astype(np.float32)
    dft_mid = np.concatenate([cos[d // 2:d // 2 + 1], sin[1:P]]).astype(np.float32)
    own = (np.arange(d) // 32)[:, None] == np.arange(16)[None, :]
    head = np.arange(P) // 32
    consts = np.concatenate([np.eye(P), head[:, None] == head[None, :], np.ones((P, P)),
                             own.reshape(4, P, 16).transpose(1, 0, 2).reshape(P, 64)], axis=1).astype(np.float32)
    return dft, dft_mid, np.ascontiguousarray(consts), np.ascontiguousarray(own.T.astype(np.float32))


def kernel(**inputs):
    import numpy as np
    import concourse.bacc as bacc
    from concourse.bass_utils import run_bass_kernel_spmd

    a = {k[3:]: np.asarray(v) for k, v in inputs.items()}
    x = np.ascontiguousarray(a["attn_input_tensor"]).reshape(-1, 512)
    dft, dft_mid, consts, spread_f = constants()
    arrays = {"x": x}
    for n, key in (("wq", "attn_Wq"), ("wk", "attn_Wk"), ("wv", "attn_Wv"), ("wd", "attn_Wd")):
        arrays[n] = np.ascontiguousarray(a[key].T)
    arrays["bq"] = np.ascontiguousarray(a["attn_bq"].reshape(4, P).T)
    for n, key in (("bk", "attn_bk"), ("bv", "attn_bv"), ("bd", "attn_bd"), ("gamma", "attn_gamma"), ("beta", "attn_beta"),
                   ("wr", "ffn_w_freq_real"), ("wi", "ffn_w_freq_imag"), ("fbias", "ffn_bias")):
        arrays[n] = np.ascontiguousarray(a[key])
    folded_order = np.concatenate([np.arange(257), np.arange(511, 256, -1)])
    for n in ("wr", "wi"):
        arrays[n] = np.ascontiguousarray(arrays[n][:, folded_order])
    arrays["dft"], arrays["dft_mid"], arrays["consts"], arrays["spread_f"] = dft, dft_mid, consts, spread_f

    nc = bacc.Bacc("TRN2", target_bir_lowering=False, num_devices=1)
    aps = {n: nc.dram_tensor(f"{n}_dram", v.shape, F32, kind="ExternalInput").ap() for n, v in arrays.items()}
    out = nc.dram_tensor("out_dram", x.shape, F32, kind="ExternalOutput").ap()
    build(nc, out=out, **aps)
    r = run_bass_kernel_spmd(nc, [{f"{n}_dram": v for n, v in arrays.items()}], core_ids=[0])
    return r.results[0]["out_dram"].reshape(8, 2048, 512)
```
